# Optimizing a Trainium2 kernel written in Bass

```python
import numpy as np
import jax
import jax.numpy as jnp

def _softmax(x, axis=-1):
    return jax.nn.softmax(x, axis=axis)

def _gelu(x):
    return jax.nn.gelu(x, approximate=True)

def _silu(x):
    return jax.nn.silu(x)

def _sigmoid(x):
    return jax.nn.sigmoid(x)

def _layernorm(x, axis=-1, eps=1e-05):
    m = jnp.mean(x, axis=axis, keepdims=True)
    v = jnp.var(x, axis=axis, keepdims=True)
    return (x - m) / jnp.sqrt(v + eps)

def _scatter_add(tgt, idx, src, axis=0):
    return tgt.at[idx].add(src)

def _segment_sum(src, seg, n):
    return jax.ops.segment_sum(src, seg, n)
kernel_name = 'mk_conv_attn_hybrid_d2_conv_nhwc384_r4_77bb5d'

def setup_inputs(seed: int=0):
    np.random.seed(seed)
    _w = jnp.asarray

    def _rec_inputs():
        import jax
        import jax.numpy as jnp
        _gk = jax.random.key(seed)
        x = -0.0005963 + 1.001 * jax.random.normal(jax.random.fold_in(_gk, 1), (8, 32, 32, 96), jnp.float32)
        return x
    x = _rec_inputs()

    def _L0_conv_setup():
        import jax, jax.numpy as jnp
        import numpy as np
        B, H, W, D = (8, 32, 32, 96)
        E, HID, O = (8, 384, 96)
        TOP_K = 2
        key = jax.random.key(seed)
        ks = jax.random.split(key, 5)
        x = jax.random.normal(ks[0], (B, H, W, D), dtype=jnp.float32)
        Wg = 0.02 * jax.random.normal(ks[1], (D, E), dtype=jnp.float32)
        bg = jnp.zeros((E,), dtype=jnp.float32)
        W1 = 0.02 * jax.random.normal(ks[2], (E, D, HID), dtype=jnp.float32)
        b1 = jnp.zeros((E, HID), dtype=jnp.float32)
        W2 = 0.02 * jax.random.normal(ks[3], (E, HID, O), dtype=jnp.float32)
        b2 = jnp.zeros((E, O), dtype=jnp.float32)
        return {'x': x, 'Wg': Wg, 'bg': bg, 'W1': W1, 'b1': b1, 'W2': W2, 'b2': b2}
    _L0_conv_all = _L0_conv_setup()
    _L0_conv_in = {k: v for k, v in _L0_conv_all.items() if k in ('Wg', 'bg', 'W1', 'b1', 'W2', 'b2')}
    del _L0_conv_all

    def _L1_attn_setup():
        import jax, jax.numpy as jnp
        import numpy as np
        N_EMBD = 96
        N_HEAD = 6
        BLOCK_SIZE = 64
        key = jax.random.key(seed)
        ks = jax.random.split(key, 5)
        B, T = (32, 64)
        x = jax.random.normal(ks[0], (B, T, N_EMBD), dtype=jnp.float32)
        w_attn = jax.random.normal(ks[1], (3 * N_EMBD, N_EMBD), dtype=jnp.float32) * (1.0 / np.sqrt(N_EMBD))
        b_attn = jax.random.normal(ks[2], (3 * N_EMBD,), dtype=jnp.float32) * 0.02
        w_proj = jax.random.normal(ks[3], (N_EMBD, N_EMBD), dtype=jnp.float32) * (1.0 / np.sqrt(N_EMBD))
        b_proj = jax.random.normal(ks[4], (N_EMBD,), dtype=jnp.float32) * 0.02
        return {'x': x, 'w_attn': w_attn, 'b_attn': b_attn, 'w_proj': w_proj, 'b_proj': b_proj}
    _L1_attn_all = _L1_attn_setup()
    _L1_attn_in = {k: v for k, v in _L1_attn_all.items() if k in ('w_attn', 'b_attn', 'w_proj', 'b_proj')}
    del _L1_attn_all

    def _L1_ffn_setup():
        import jax, jax.numpy as jnp
        import numpy as np
        NUM_EXPERTS = 4
        TOP_K = 2
        DIM = 96
        HID = 4 * DIM
        key = jax.random.key(seed)
        ks = jax.random.split(key, 5)
        B, S = (16, 512)
        scale_in = 1.0 / np.sqrt(DIM)
        scale_hid = 1.0 / np.sqrt(HID)
        return {'x': jax.random.normal(ks[0], (B, S, DIM), dtype=jnp.float32), 'gate_w': jax.random.normal(ks[1], (DIM, NUM_EXPERTS), dtype=jnp.float32) * scale_in, 'gate_b': jnp.zeros((NUM_EXPERTS,), dtype=jnp.float32), 'w1': jax.random.normal(ks[2], (NUM_EXPERTS, DIM, HID), dtype=jnp.float32) * scale_in, 'b1': jnp.zeros((NUM_EXPERTS, HID), dtype=jnp.float32), 'w2': jax.random.normal(ks[3], (NUM_EXPERTS, HID, DIM), dtype=jnp.float32) * scale_hid, 'b2': jnp.zeros((NUM_EXPERTS, DIM), dtype=jnp.float32)}
    _L1_ffn_all = _L1_ffn_setup()
    _L1_ffn_in = {k: v for k, v in _L1_ffn_all.items() if k in ('gate_w', 'gate_b', 'w1', 'b1', 'w2', 'b2')}
    del _L1_ffn_all
    return {'x': x, 'L0_conv_Wg': _L0_conv_in['Wg'], 'L0_conv_bg': _L0_conv_in['bg'], 'L0_conv_W1': _L0_conv_in['W1'], 'L0_conv_b1': _L0_conv_in['b1'], 'L0_conv_W2': _L0_conv_in['W2'], 'L0_conv_b2': _L0_conv_in['b2'], 'L1_attn_w_attn': _L1_attn_in['w_attn'], 'L1_attn_b_attn': _L1_attn_in['b_attn'], 'L1_attn_w_proj': _L1_attn_in['w_proj'], 'L1_attn_b_proj': _L1_attn_in['b_proj'], 'L1_ffn_gate_w': _L1_ffn_in['gate_w'], 'L1_ffn_gate_b': _L1_ffn_in['gate_b'], 'L1_ffn_w1': _L1_ffn_in['w1'], 'L1_ffn_b1': _L1_ffn_in['b1'], 'L1_ffn_w2': _L1_ffn_in['w2'], 'L1_ffn_b2': _L1_ffn_in['b2']}

def reference(x, L0_conv_Wg, L0_conv_bg, L0_conv_W1, L0_conv_b1, L0_conv_W2, L0_conv_b2, L1_attn_w_attn, L1_attn_b_attn, L1_attn_w_proj, L1_attn_b_proj, L1_ffn_gate_w, L1_ffn_gate_b, L1_ffn_w1, L1_ffn_b1, L1_ffn_w2, L1_ffn_b2):
    import jax
    import jax.numpy as jnp

    def _L0_conv_ref(x, Wg, bg, W1, b1, W2, b2):
        import jax, jax.numpy as jnp
        import numpy as np
        B, H, W, D = (8, 32, 32, 96)
        E, HID, O = (8, 384, 96)
        TOP_K = 2
        logits = jnp.einsum('bhwd,de->bhwe', x, Wg) + bg
        _, top_idx = jax.lax.top_k(logits, TOP_K)
        sel = jnp.sum(jax.nn.one_hot(top_idx, E, dtype=jnp.float32), axis=-2) > 0
        sparse_logits = jnp.where(sel, logits, -jnp.inf)
        gates = jax.nn.softmax(sparse_logits, axis=-1)
        h = jnp.einsum('bhwd,edf->bhwef', x, W1) + b1
        h = jax.nn.gelu(h, approximate=False)
        y = jnp.einsum('bhwef,efo->bhweo', h, W2) + b2
        out = jnp.einsum('bhweo,bhwe->bhwo', y, gates)
        return out

    def _L1_attn_ref(x, w_attn, b_attn, w_proj, b_proj):
        import jax, jax.numpy as jnp
        import numpy as np
        N_EMBD = 96
        N_HEAD = 6
        BLOCK_SIZE = 64
        B, T, C = x.shape
        hd = C // N_HEAD
        qkv = x @ w_attn.T + b_attn
        q, k, v = jnp.split(qkv, 3, axis=2)
        q = q.reshape(B, T, N_HEAD, hd).transpose(0, 2, 1, 3)
        k = k.reshape(B, T, N_HEAD, hd).transpose(0, 2, 1, 3)
        v = v.reshape(B, T, N_HEAD, hd).transpose(0, 2, 1, 3)
        att = jnp.einsum('bhqd,bhkd->bhqk', q, k) * (1.0 / np.sqrt(hd))
        causal = jnp.tril(jnp.ones((T, T), dtype=bool))
        att = jnp.where(causal, att, -jnp.inf)
        att = jax.nn.softmax(att, axis=-1)
        y = jnp.einsum('bhqk,bhkd->bhqd', att, v)
        y = y.transpose(0, 2, 1, 3).reshape(B, T, C)
        return y @ w_proj.T + b_proj

    def _L1_ffn_ref(x, gate_w, gate_b, w1, b1, w2, b2):
        import jax, jax.numpy as jnp
        import numpy as np
        NUM_EXPERTS = 4
        TOP_K = 2
        DIM = 96
        HID = 4 * DIM
        scores = jnp.einsum('bsd,de->bse', x, gate_w) + gate_b
        probs = jax.nn.softmax(scores, axis=-1)
        topk_vals, topk_idx = jax.lax.top_k(probs, TOP_K)
        mask = jnp.sum(jax.nn.one_hot(topk_idx, NUM_EXPERTS, dtype=probs.dtype), axis=-2)
        masked = probs * mask
        masked = masked / (jnp.sum(masked, axis=-1, keepdims=True) + 1e-09)
        h = jax.nn.gelu(jnp.einsum('bsd,edh->ebsh', x, w1) + b1[:, None, None, :], approximate=False)
        y = jnp.einsum('ebsh,ehd->ebsd', h, w2) + b2[:, None, None, :]
        out = jnp.einsum('bse,ebsd->bsd', masked, y)
        return out

    def _gn(v, G=32, eps=1e-05):
        B_, H_, W_, C_ = v.shape
        g = v.reshape(B_, H_, W_, G, C_ // G)
        m = jnp.mean(g, axis=(1, 2, 4), keepdims=True)
        s = jnp.var(g, axis=(1, 2, 4), keepdims=True)
        return ((g - m) / jnp.sqrt(s + eps)).reshape(v.shape)

    def _ln_c(v, eps=1e-06):
        m = jnp.mean(v, axis=-1, keepdims=True)
        s = jnp.var(v, axis=-1, keepdims=True)
        return (v - m) / jnp.sqrt(s + eps)

    def _ln_t(v, eps=1e-05):
        m = jnp.mean(v, axis=-1, keepdims=True)
        s = jnp.var(v, axis=-1, keepdims=True)
        return (v - m) / jnp.sqrt(s + eps)

    def _to_tokens(v):
        B_, H_, W_, C_ = v.shape
        return v.reshape(B_, H_ * W_, C_)

    def _from_tokens(t, like):
        return t.reshape(like.shape)
    x = x + _L0_conv_ref(_gn(x), L0_conv_Wg, L0_conv_bg, L0_conv_W1, L0_conv_b1, L0_conv_W2, L0_conv_b2)
    t = _to_tokens(x)
    t = t + _L1_attn_ref(_ln_t(t), L1_attn_w_attn, L1_attn_b_attn, L1_attn_w_proj, L1_attn_b_proj)
    t = t + _L1_ffn_ref(_ln_t(t), L1_ffn_gate_w, L1_ffn_gate_b, L1_ffn_w1, L1_ffn_b1, L1_ffn_w2, L1_ffn_b2)
    x = _from_tokens(t, x)
    return x

_drawn_inputs = setup_inputs


def setup_inputs(seed=0):
    import zlib

    import numpy as np

    out = dict(_drawn_inputs(seed))
    spreads = {'L0_conv_bg': (0.0, 0.1),
     'L0_conv_b1': (0.0, 0.1),
     'L0_conv_b2': (0.0, 0.1),
     'L1_ffn_gate_b': (0.0, 0.1),
     'L1_ffn_b1': (0.0, 0.1),
     'L1_ffn_b2': (0.0, 0.1)}
    factors = {}
    for name, (base, spread) in spreads.items():
        noise = np.random.default_rng([zlib.crc32(name.encode()), seed]).standard_normal(out[name].shape)
        drawn = base * np.exp(spread * noise) if base else spread * noise
        out[name] = jnp.asarray(drawn.astype(out[name].dtype))
    for name, factor in factors.items():
        out[name] = (out[name] * factor).astype(out[name].dtype)
    return out
```

```python
from contextlib import ExitStack

import concourse.bass as bass
from concourse import mybir

F32 = mybir.dt.float32
F16 = mybir.dt.float16
BF16 = mybir.dt.bfloat16
I32 = mybir.dt.int32
U32 = mybir.dt.uint32
ALU = mybir.AluOpType
ACT = mybir.ActivationFunctionType
AX = mybir.AxisListType.X

P = 128
NIMG, T, D = 8, 1024, 96
TT = T // P
CH = 512
NC = T // CH
TC = CH // P
HID = 384
HT = HID // P
EA, EC = 8, 4
NE = EA + EC
H, HD = 6, 16
TR = 3
ONE = D
WS = 64.0
MS = 256.0
MROW = 96
NEG = -1.0e30
GA, GC = NC * EA, NC * EC
MAXU = H * (TC + 2 * TC)
STEPS = 2 * (TC + 2 * TC)
SU = STEPS * TR
FIRST_LOOP, END_LOOP = 3, NIMG - 1
M_SETUP = 5
M_GN = 8
M_FRONT = 9
M_PROJ = 2
M_C = 2 + 1 + 1 + 2
M_ITER = M_GN + M_FRONT + M_PROJ + M_C


class Count:

    def __init__(self, per):
        self.per, self.it, self.k = per, None, 0

    def enter(self, it):
        self.at_entry = self.k
        self.it, self.k = it, self.k - FIRST_LOOP * self.per

    def leave(self):
        n = self.k + FIRST_LOOP * self.per - self.at_entry
        assert n == self.per, (n, self.per)
        self.it, self.k = None, self.at_entry + (END_LOOP - FIRST_LOOP) * self.per

    def value(self, times=1, plus=0):
        k = self.k * times + plus
        return k if self.it is None else self.it * (self.per * times) + k


class Image:

    def __init__(self, it, off):
        self.it, self.off = it, off

    def value(self, per, k):
        return self.it * per + (self.off * per + k)


def wait(eng, sem, value):
    if not isinstance(value, int) or value > 0:
        eng.wait_ge(sem, value)


def walk(eng, counts, iteration):
    for it in range(FIRST_LOOP):
        iteration(it, True, it >= 1, it >= 2)
    with eng.Fori(FIRST_LOOP, END_LOOP) as it:
        for c in counts:
            c.enter(it)
        iteration(it, True, True, True)
    for c in counts:
        c.leave()
    iteration(NIMG - 1, True, True, True)
    iteration(NIMG, False, True, True)
    iteration(NIMG + 1, False, False, True)


def has_next(it):
    return not isinstance(it, int) or it + 1 < NIMG


def front_slots(g):
    first, last = 4, GA
    if g < first:
        return range(0)
    n = last + 1 - first
    return range(MAXU * (g - first) // n, MAXU * (g - first + 1) // n)


MAX_UNITS = [(h, i, part) for h in range(H) for i in range(TT) for part in range(1 if i < TC else 2)]
SOFT_STEPS = [(t, c, j) for t in range(2) for c in range(NC) for j in range(TC * (c + 1))]


def build(nc, x, cWg, cbg, cW1, cb1, cW2, cb2, w_attn, b_attn, w_proj, b_proj,
          fWg, fbg, fW1, fb1, fW2, fb2, out):
    nc.disable_value_cache = True
    with ExitStack() as ctx:
        def sb(name, shape, dt=F32):
            return ctx.enter_context(nc.sbuf_tensor(name, shape, dt))

        def sem(name):
            return ctx.enter_context(nc.semaphore(name))

        w1_raw = sb("w1_raw", [ONE + 1, NE * HID])
        w1h = sb("w1h", [ONE + 1, NE * HID], F16)
        w1l = sb("w1l", [ONE + 1, NE * HID], F16)
        w2 = sb("w2", [P, NE * HT, D])
        wg_raw = sb("wg_raw", [ONE + 1, NE])
        wgh = sb("wgh", [ONE + 1, NE], F16)
        wgl = sb("wgl", [ONE + 1, NE], F16)
        b2a = sb("b2a", [P, TT, D])
        b2c = sb("b2c", [P, TT, D])
        watt = sb("watt", [D, 3, D])
        batt = sb("batt", [ONE + 1, 3 * D])
        wqh = sb("wqh", [ONE + 1, 3 * D], F16)
        wql = sb("wql", [ONE + 1, 3 * D], F16)
        wpad = sb("wpad", [D, 2, TR, 32])
        wp = sb("wp", [D, 2, D])
        ident = sb("ident", [P, P])
        identb = sb("identb", [P, P], BF16)
        mask_q = sb("mask_q", [P, P], BF16)
        mask_k = sb("mask_k", [P, P], BF16)
        group = sb("group", [D, D])
        expert = sb("expert", [P, TT, 8], I32)
        power = sb("power", [P, TT])
        epsilon = sb("epsilon", [P, TT])

        xin = sb("xin", [P, TT, D])
        xt = sb("xt", [D, T])
        gst = sb("gst", [D, NC, 6])
        gmv = sb("gmv", [D, 2])
        gmean = sb("gmean", [D, 1])
        gdev = sb("gdev", [D, 1])
        gspread = sb("gspread", [D, 1])
        gvar = sb("gvar", [D, 1])
        grstd = sb("grstd", [D, 1])
        xah = sb("xah", [ONE + 1, T], F16)
        xal = sb("xal", [ONE + 1, T], F16)
        acc = sb("acc", [P, TT, D])
        x1 = sb("x1", [P, TT, D])
        hid = sb("hid", [P, 2, HT, CH])

        class Routing:
            def __init__(self, n):
                self.score = sb(f"score{n}", [P, TT, 8])
                self.top = sb(f"top{n}", [P, TT, 8])
                self.idx = sb(f"idx{n}", [P, TT, 8], U32)
                self.shifted = sb(f"shifted{n}", [P, TT, 8])
                self.ex = sb(f"ex{n}", [P, TT, 8])
                self.prob = sb(f"prob{n}", [P, TT, 8])
                self.first = sb(f"first{n}", [P, TT, 8])
                self.second = sb(f"second{n}", [P, TT, 8])
                self.total = sb(f"total{n}", [P, TT])
                self.inv = sb(f"inv{n}", [P, TT])
                self.gates = sb(f"gates{n}", [P, 2 * TT, 8])
                self.gt = sb(f"gt{n}", [P, P])

        ra, rc_ = Routing("a"), Routing("c")

        st = sb("st", [P, TT, 6])
        mv1 = sb("mv1", [P, TT, 2])
        mv2 = sb("mv2", [P, TT, 2])
        rstd1 = sb("rstd1", [P, TT])
        rstd2 = sb("rstd2", [P, TT])
        xn1 = sb("xn1", [P, TT, D])
        xn2 = sb("xn2", [P, TT, D])
        xbh = sb("xbh", [ONE + 1, T], F16)
        xbl = sb("xbl", [ONE + 1, T], F16)
        qk_h = sb("qk_h", [D, 2, T], F16)
        qk_l = sb("qk_l", [D, 2, T], F16)
        qs = sb("qs", [MROW + 2, H, T], F16)
        ks = sb("ks", [MROW + 2, H, T], F16)
        vaug = sb("vaug", [P, TT, H, 32])
        mpart = sb("mpart", [P, H, TT, 2])
        mneg = sb("mneg", [P, P])
        mth = sb("mth", [H * TT, P], F16)
        mtl = sb("mtl", [H * TT, P], F16)
        probs = sb("probs", [P, 2, TR, CH])
        yt = sb("yt", [D, 2, T])
        sums = sb("sums", [H * TT, P])
        rsum = sb("rsum", [H * TT, P])
        rb = sb("rb", [D, 2, T])
        x1r = sb("x1r", [P, TT, D])

        x2 = sb("x2", [P, TT, D])
        xch = sb("xch", [ONE + 1, T], F16)
        xcl = sb("xcl", [ONE + 1, T], F16)
        xo = sb("xo", [P, TT, D])

        rsum_dram = nc.dram_tensor("rsum_dram", (H, T), F32, kind="Internal").ap()

        ps_u = [ctx.enter_context(nc.psum_tensor(f"ps_u{i}", [P, CH], F32)) for i in range(2)]
        ps_y = [ctx.enter_context(nc.psum_tensor(f"ps_y{i}", [P, CH], F32)) for i in range(2)]
        ps_r = [ctx.enter_context(nc.psum_tensor(f"ps_r{i}", [P, CH], F32)) for i in range(3)]
        ps_m = ctx.enter_context(nc.psum_tensor("ps_m", [P, CH], F32))

        w_loaded = [sem(f"w_loaded{i}") for i in range(7)]
        zeroed = sem("zeroed")
        consts = sem("consts")
        w_ready = sem("w_ready")
        m_full, m_free = sem("m_full"), sem("m_free")
        up_full, h_ready = sem("up_full"), sem("h_ready")
        y_full, y_free = sem("y_full"), sem("y_free")
        mx_full, mx_free = sem("mx_full"), sem("mx_free")
        s_full, p_ready = sem("s_full"), sem("p_ready")
        pv_step = sem("pv_step")
        pv_free = sem("pv_free")
        x_loaded = sem("x_loaded")
        xt_free = sem("xt_free")
        gn_var, gn_rstd = sem("gn_var"), sem("gn_rstd")
        ln1_var, ln1_rstd = sem("ln1_var"), sem("ln1_rstd")
        ln2_var, ln2_rstd = sem("ln2_var"), sem("ln2_rstd")
        gn_in = sem("gn_in")
        xn1_ready, xn2_ready = sem("xn1_ready"), sem("xn2_ready")
        xb_ready, xc_ready = sem("xb_ready"), sem("xc_ready")
        sub_a, exp_a, gates_a, gt_a = sem("sub_a"), sem("exp_a"), sem("gates_a"), sem("gt_a")
        sub_c, exp_c, gates_c, gt_c = sem("sub_c"), sem("exp_c"), sem("gates_c"), sem("gt_c")
        acc_ready = sem("acc_ready")
        qk_split, qk_stacked, v_ready = sem("qk_split"), sem("qk_stacked"), sem("v_ready")
        mneg_ready, m_split, m_stacked = sem("mneg_ready"), sem("m_split"), sem("m_stacked")
        yt_ready, sums_in, rsum_ready = sem("yt_ready"), sem("sums_in"), sem("rsum_ready")
        rsum_out, rb_in, yn_ready = sem("rsum_out"), sem("rb_in"), sem("yn_ready")
        x2_ready, x1r_ready = sem("x2_ready"), sem("x1r_ready")
        xo_ready, out_done = sem("xo_ready"), sem("out_done")

        QK_DMAS = 2 * 3 * H

        x_d = x.rearrange("b (t q) w c -> b (q w) t c", t=TT)
        out_d = out.rearrange("b (t q) w c -> b (q w) t c", t=TT)

        block = ctx.enter_context(nc.Block())

        @block.sync
        def _(sp):
            sp.wait_ge(zeroed, 1)
            sp.dma_start(wg_raw[0:D, 0:EA], cWg).then_inc(w_loaded[0], 16)
            sp.dma_start(wg_raw[D:D + 1, 0:EA], cbg.rearrange("(a e) -> a e", a=1)).then_inc(w_loaded[0], 16)
            sp.dma_start(wg_raw[0:D, EA:NE], fWg).then_inc(w_loaded[0], 16)
            sp.dma_start(wg_raw[D:D + 1, EA:NE], fbg.rearrange("(a e) -> a e", a=1)).then_inc(w_loaded[0], 16)
            raw = w1_raw[:].rearrange("d (e f) -> d e f", e=NE)
            sp.dma_start(raw[0:D, 0:EA, :], cW1.rearrange("e d f -> d e f")).then_inc(w_loaded[1], 16)
            sp.dma_start(raw[D:D + 1, 0:EA, :], cb1.rearrange("(a e) f -> a e f", a=1)).then_inc(w_loaded[1], 16)
            sp.dma_start(raw[0:D, EA:NE, :], fW1.rearrange("e d f -> d e f")).then_inc(w_loaded[1], 16)
            sp.dma_start(raw[D:D + 1, EA:NE, :], fb1.rearrange("(a e) f -> a e f", a=1)).then_inc(w_loaded[1], 16)
            for t in range(TT):
                sp.dma_start(b2a[8 * t:8 * t + EA, t, :], cb2).then_inc(w_loaded[2], 16)
                sp.dma_start(b2c[8 * t:8 * t + EC, t, :], fb2).then_inc(w_loaded[2], 16)
            sp.dma_start(w2[:, 0:EA * HT, :], cW2.rearrange("e (j p) o -> p (e j) o", p=P)).then_inc(w_loaded[3], 16)
            sp.dma_start(w2[:, EA * HT:, :], fW2.rearrange("e (j p) o -> p (e j) o", p=P)).then_inc(w_loaded[4], 16)
            sp.dma_start(watt[:], w_attn.rearrange("(s o) i -> o s i", s=3)).then_inc(w_loaded[5], 16)
            sp.dma_start(batt[D:D + 1, :], b_attn.rearrange("(a o) -> a o", a=1)).then_inc(w_loaded[5], 16)
            for t in range(2):
                sp.dma_start(wpad[:, t, :, 0:HD],
                             w_proj[:, t * TR * HD:(t + 1) * TR * HD].rearrange("o (g d) -> o g d", g=TR)
                             ).then_inc(w_loaded[6], 16)
            sp.dma_start(wpad[:, 0, 0, HD:HD + 1], b_proj.rearrange("(o a) -> o a", a=1)).then_inc(w_loaded[6], 16)

            def stack_qk(b):
                wait(sp, s_full, b.value(SU, 0))
                wait(sp, qk_split, b.value(1, 1))
                for dst, s, parts in ((qs, 0, (qk_h, qk_l, qk_h)), (ks, 1, (qk_h, qk_h, qk_l))):
                    for n, part in enumerate(parts):
                        for h in range(H):
                            sp.dma_start(dst[HD * n:HD * (n + 1), h, :], part[HD * h:HD * (h + 1), s, :]
                                         ).then_inc(qk_stacked, 16)

            def stack_maxima(b):
                wait(sp, m_split, b.value(1, 1))
                for n, part in enumerate((mth, mtl)):
                    sp.dma_start(qs[MROW + n:MROW + n + 1, :, :].rearrange("a h (i q) -> a (h i) q", q=P),
                                 part[:]).then_inc(m_stacked, 16)

            def spread_sums(b):
                wait(sp, yt_ready, b.value(1, 1))
                for t in range(2):
                    for g in range(TR):
                        n = (t * TR + g) * TT
                        sp.dma_start(sums[n:n + TT, :], yt[32 * g + HD:32 * g + HD + 1, t, :]
                                     .rearrange("a (i q) -> a i q", q=P)).then_inc(sums_in, 16)
                wait(sp, rsum_ready, b.value(1, 1))
                sp.dma_start(rsum_dram.rearrange("h (i q) -> (h i) q", q=P), rsum[:]).then_inc(rsum_out, 16)
                wait(sp, rsum_out, b.value(16, 16))
                for t in range(2):
                    for g in range(TR):
                        h = t * TR + g
                        sp.dma_start(rb[32 * g:32 * g + 32, t, :],
                                     rsum_dram[h:h + 1, :].partition_broadcast(32)).then_inc(rb_in, 16)

            def iteration(it, moe_a, attend, moe_c):
                if attend:
                    b = Image(it, -1)
                    stack_qk(b)
                    stack_maxima(b)
                    spread_sums(b)

            walk(sp, [], iteration)

        @block.gpsimd
        def _(pool):
            g = nc.gpsimd
            for tile, value in ((b2a, 0.0), (b2c, 0.0), (wpad, 0.0), (qs, 0.0), (ks, 0.0), (vaug, 0.0),
                                (mpart, NEG), (mneg, 0.0), (epsilon, 1e-5), (ra.gates, 0.0), (rc_.gates, 0.0), (rc_.prob, -1.0),
                                (power, -0.5), (xal, 0.0), (xbl, 0.0), (xcl, 0.0)):
                g.memset(tile[:], value)
            pool.drain()
            g.memset(vaug[:, :, :, HD:HD + 1], 1.0)
            for tile, value in ((ks[MROW:MROW + 2, :, :], MS), (xah[ONE:ONE + 1, :], 1.0),
                                (xbh[ONE:ONE + 1, :], 1.0), (xch[ONE:ONE + 1, :], 1.0)):
                pool.drain()
                g.memset(tile, value)
            pool.drain().then_inc(zeroed, 1)
            g.memset(ident[:], 0.0)
            g.memset(identb[:], 0.0)
            g.memset(mask_q[:], 0.0)
            g.memset(mask_k[:], 0.0)
            g.memset(group[:], 1.0 / 3.0)
            g.iota(expert[:], pattern=[[0, TT], [1, 8]], base=0, channel_multiplier=0)
            pool.drain()
            for tile in (ident, identb):
                g.affine_select(out=tile[:], in_=tile[:], compare_op=ALU.not_equal, fill=1.0, base=0,
                                pattern=[[-1, P]], channel_multiplier=1)
            g.affine_select(out=mask_q[:], in_=mask_q[:], compare_op=ALU.is_ge, fill=NEG, base=0,
                            pattern=[[-1, P]], channel_multiplier=1)
            g.affine_select(out=mask_k[:], in_=mask_k[:], compare_op=ALU.is_ge, fill=NEG, base=0,
                            pattern=[[1, P]], channel_multiplier=-1)
            grouped = group[:].rearrange("p (a r) -> p a r", r=3)
            g.affine_select(out=grouped, in_=grouped, compare_op=ALU.is_ge, fill=0.0, base=0,
                            pattern=[[-3, D // 3], [0, 3]], channel_multiplier=1)
            pool.drain()
            g.affine_select(out=grouped, in_=grouped, compare_op=ALU.is_ge, fill=0.0, base=2,
                            pattern=[[3, D // 3], [0, 3]], channel_multiplier=-1)
            pool.drain().then_inc(consts, 1)

            def rstd(dst, var, ready, done, b):
                pool.wait_ge(ready, b.value(1, 1))
                n = var.shape[0]
                g.tensor_tensor(dst, var, epsilon[0:n, 0:dst.shape[1]], ALU.add)
                pool.drain()
                g.tensor_tensor(dst, dst, power[0:n, 0:dst.shape[1]], ALU.pow).then_inc(done, 1)

            def iteration(it, moe_a, attend, moe_c):
                if moe_c:
                    rstd(rstd2[:], mv2[:, :, 1], ln2_var, ln2_rstd, Image(it, -2))
                if has_next(it):
                    rstd(grstd[:], gvar[:], gn_var, gn_rstd, Image(it, 1))
                if moe_a:
                    rstd(rstd1[:], mv1[:, :, 1], ln1_var, ln1_rstd, Image(it, 0))

            rstd(grstd[:], gvar[:], gn_var, gn_rstd, Image(0, 0))
            walk(pool, [], iteration)

        @block.tensor
        def _(pe):
            m, grp = Count(M_ITER), Count(GA + GC)

            def mm(dst, lhsT, rhs, start=True, stop=True):
                return nc.tensor.matmul(dst, lhsT, rhs, start=start, stop=stop, skip_group_check=True)

            def split(dst, wh, wl, xh, xl, moving_x):
                pairs = ((wh, xh), (wl, xh), (wh, xl))
                for n, (w, v) in enumerate(pairs):
                    a, b = (w, v) if moving_x else (v, w)
                    last = mm(dst, a, b, n == 0, n == 2)
                return last

            def shared():
                wait(pe, m_free, m.value())
                m.k += 1

            def turn(src, b_ready):
                for c in range(NC):
                    shared()
                    for i in range(TC):
                        last = nc.tensor.transpose(ps_m[0:D, P * i:P * (i + 1)], src[:, TC * c + i, :], ident[:])
                    last.then_inc(m_full, 1)

            def logits(xh, xl, e0, n):
                shared()
                for t in range(TT):
                    tok = slice(P * t, P * (t + 1))
                    last = split(ps_m[:, 8 * t:8 * t + n], wgh[:, e0:e0 + n], wgl[:, e0:e0 + n],
                                 xh[:, tok], xl[:, tok], False)
                last.then_inc(m_full, 1)

            def gates_turn(r, ready, b):
                pe.wait_ge(ready, b.value(1, 1))
                shared()
                nc.tensor.transpose(ps_m[:, 0:P], r.gates[:].rearrange("p t e -> p (t e)"), ident[:]
                                    ).then_inc(m_full, 1)

            def bias2(r, b2, ready, b):
                pe.wait_ge(ready, b.value(1, 1))
                for c in range(NC):
                    shared()
                    mm(ps_m[:, 0:TC * D], r.gt[:],
                       b2[:, TC * c:TC * (c + 1), :].rearrange("p t d -> p (t d)")).then_inc(m_full, 1)

            def gn(part, b):
                if part == 0:
                    pe.wait_ge(x_loaded, b.value(16, 16))
                    turn(xin, None)
                if part in (1, 2):
                    pe.wait_ge(gn_in, b.value(2, part))
                    shared()
                    mm(ps_m[0:D, 0:1], group[:], gmv[:, 0:1] if part == 1 else gspread[:]).then_inc(m_full, 1)
                if part == 3:
                    pe.wait_ge(xt_free, b.value(1, 1))
                    logits(xah, xal, 0, EA)
                if part == 4:
                    gates_turn(ra, gates_a, b)
                if part == 5:
                    bias2(ra, b2a, gt_a, b)

            def up(xh, xl, e, c, j):
                wait(pe, h_ready, grp.value(HT, j - 1))
                w = slice((e * HT + j) * P, (e * HT + j + 1) * P)
                tok = slice(CH * c, CH * (c + 1))
                bank = ps_u[(HT * grp.k + j) % 2]
                split(bank[:], w1h[:, w], w1l[:, w], xh[:, tok], xl[:, tok], True).then_inc(up_full, 1)

            def down(e, i):
                if i == 0:
                    pe.wait_ge(h_ready, grp.value(HT, 0))
                    wait(pe, y_free, grp.value(1, -2))
                n = grp.k - 1
                for j in range(HT):
                    last = mm(ps_y[n % 2][:, D * i:D * (i + 1)], hid[:, n % 2, j, P * i:P * (i + 1)],
                              w2[:, e * HT + j, :], j == 0, j == HT - 1)
                if i == TC - 1:
                    last.then_inc(y_full, 1)

            def moe(xh, xl, e0, ne, between):
                for g in range(NC * ne + 1):
                    for j in range(TC):
                        if j < HT and g < NC * ne:
                            up(xh, xl, e0 + g % ne, g // ne, j)
                        if g > 0:
                            down(e0 + (g - 1) % ne, j)
                    if g < NC * ne:
                        grp.k += 1
                    between(g)

            def qkv(b):
                pe.wait_ge(xb_ready, b.value(1, 1))
                for s in range(2):
                    w = slice(D * s, D * (s + 1))
                    for c in range(NC):
                        shared()
                        tok = slice(CH * c, CH * (c + 1))
                        split(ps_m[0:D, :], wqh[:, w], wql[:, w], xbh[:, tok], xbl[:, tok], True
                              ).then_inc(m_full, 1)

            def values():
                w = slice(2 * D, 3 * D)
                for c in range(NC):
                    shared()
                    for i in range(TC):
                        tok = slice(P * (TC * c + i), P * (TC * c + i + 1))
                        last = split(ps_m[:, D * i:D * (i + 1)], wqh[:, w], wql[:, w], xbh[:, tok], xbl[:, tok],
                                     False)
                    last.then_inc(m_full, 1)

            def maximum(b, k):
                h, i, part = MAX_UNITS[k]
                if k == 0:
                    pe.wait_ge(qk_stacked, b.value(16 * QK_DMAS, 16 * QK_DMAS))
                    wait(pe, p_ready, b.value(SU, 0))
                wait(pe, mx_free, b.value(MAXU, k - 2))
                k0 = CH * part
                w = min(CH, P * (i + 1) - k0)
                diagonal = k0 + w == P * (i + 1)
                bank = ps_r[k % 3]
                last = mm(bank[:, 0:w], qs[0:MROW, h, P * i:P * (i + 1)], ks[0:MROW, h, k0:k0 + w],
                          True, not diagonal)
                if diagonal:
                    last = mm(bank[:, w - P:w], identb[:], mask_q[:], False, True)
                last.then_inc(mx_full, 1)

            def maxima_turn(b):
                pe.wait_ge(mneg_ready, b.value(1, 1))
                shared()
                nc.tensor.transpose(ps_m[:, 0:P], mneg[:], ident[:]).then_inc(m_full, 1)

            def soft_scores(b, n):
                t, c, j = SOFT_STEPS[n]
                q0 = max(CH * c, P * j)
                w = CH * (c + 1) - q0
                for g in range(TR):
                    k = n * TR + g
                    if n == 0 and g == 0:
                        pe.wait_ge(m_stacked, b.value(32, 32))
                        pe.wait_ge(mx_free, b.value(MAXU, MAXU))
                    if n > 0:
                        pe.wait_ge(p_ready, b.value(SU, k - 2))
                    h = t * TR + g
                    diagonal = P * j >= CH * c
                    last = mm(ps_r[k % 3][:, 0:w], ks[0:MROW + 2, h, P * j:P * (j + 1)],
                              qs[0:MROW + 2, h, q0:q0 + w], True, not diagonal)
                    if diagonal:
                        last = mm(ps_r[k % 3][:, 0:P], identb[:], mask_k[:], False, True)
                    last.then_inc(s_full, 1)

            def soft_values(b, n):
                t, c, j = SOFT_STEPS[n]
                q0 = max(CH * c, P * j)
                w = CH * (c + 1) - q0
                off = q0 - CH * c
                pe.wait_ge(p_ready, b.value(SU, (n + 1) * TR))
                if n == 0:
                    pe.wait_ge(v_ready, b.value(NC, NC))
                if j == 0:
                    wait(pe, pv_free, b.value(4, 2 * t + c - 1))
                for g in range(TR):
                    last = mm(ps_y[(2 * t + c) % 2][32 * g:32 * g + 32, off:off + w],
                              vaug[:, j, t * TR + g, :], probs[:, n % 2, g, 0:w],
                              j == 0, j == TC * (c + 1) - 1)
                last.then_inc(pv_step, 1)

            def softmax(b):
                wait(pe, y_free, grp.value())
                for n in range(STEPS + 1):
                    if n < STEPS:
                        soft_scores(b, n)
                    if n > 0:
                        soft_values(b, n - 1)

            def project(b):
                pe.wait_ge(yn_ready, b.value(1, 1))
                for c in range(NC):
                    shared()
                    for i in range(TC):
                        q = P * (TC * c + i)
                        for t in range(2):
                            last = mm(ps_m[:, D * i:D * (i + 1)], yt[:, t, q:q + P], wp[:, t, :], t == 0, t == 1)
                    last.then_inc(m_full, 1)

            def iteration(it, moe_a, attend, moe_c):
                def in_a(g):
                    b1, b2 = Image(it, -1), Image(it, -2)
                    if g == 0 and attend:
                        pe.wait_ge(xn1_ready, b1.value(1, 1))
                        turn(xn1, None)
                    if g == 1 and attend:
                        qkv(b1)
                    if g == 2 and attend:
                        values()
                    if g == 2 and moe_c:
                        project(b2)
                    if g == 5 and moe_c:
                        pe.wait_ge(xn2_ready, b2.value(1, 1))
                        turn(xn2, None)
                    if g == 6 and moe_c:
                        pe.wait_ge(xc_ready, b2.value(1, 1))
                        logits(xch, xcl, EA, EC)
                    if g == 9 and moe_c:
                        gates_turn(rc_, gates_c, b2)
                    if g == 10 and moe_c:
                        bias2(rc_, b2c, gt_c, b2)
                    if attend:
                        for k in front_slots(g):
                            maximum(b1, k)
                    if g == GA and attend:
                        maxima_turn(b1)

                def in_c(g):
                    if has_next(it):
                        slots = {0: 0, 2: 1, 3: 2, 6: 3}
                        if g in slots:
                            gn(slots[g], Image(it, 1))

                wait(pe, pv_free, Image(it, -2).value(4, 4))
                if moe_a:
                    if isinstance(it, int) and it == 0:
                        pe.wait_ge(w_loaded[3], 16)
                    moe(xah, xal, 0, EA, in_a)
                else:
                    for g in range(GA + 1):
                        in_a(g)
                if moe_c:
                    moe(xch, xcl, EA, EC, in_c)
                else:
                    for g in range(GC + 1):
                        in_c(g)
                if has_next(it):
                    gn(4, Image(it, 1))
                    gn(5, Image(it, 1))
                if attend:
                    softmax(Image(it, -1))

            pe.wait_ge(consts, 1)
            pe.wait_ge(w_loaded[5], 32)
            for s in range(3):
                shared()
                nc.tensor.transpose(ps_m[0:D, 0:D], watt[:, s, :], ident[0:D, 0:D]).then_inc(m_full, 1)
            pe.wait_ge(w_loaded[6], 48)
            for t in range(2):
                shared()
                nc.tensor.transpose(ps_m[0:D, 0:D], wpad[:, t, :, :].rearrange("o g d -> o (g d)"),
                                    ident[0:D, 0:D]).then_inc(m_full, 1)
            pe.wait_ge(w_ready, 1)
            pe.wait_ge(w_loaded[2], 32 * TT)
            pe.wait_ge(w_loaded[4], 16)
            for part in range(6):
                gn(part, Image(0, 0))
            walk(pe, [m, grp], iteration)

        @block.scalar
        def _(act):
            m, grp = Count(M_ITER), Count(GA + GC)
            a = nc.scalar

            def moe(ne, between):
                for g in range(NC * ne + 1):
                    if g < NC * ne:
                        for j in range(HT):
                            act.wait_ge(up_full, grp.value(HT, j + 1))
                            if j == 0:
                                wait(act, y_full, grp.value(1, -1))
                            a.activation(hid[:, grp.k % 2, j, :], ps_u[(HT * grp.k + j) % 2][:], ACT.Gelu,
                                         scale=1.0 / WS).then_inc(h_ready, 1)
                        grp.k += 1
                    between(g)

            def exponentials(r, ready, done, n, b):
                act.wait_ge(ready, b.value(1, 1))
                a.activation(r.ex[:, :, 0:n], r.shifted[:, :, 0:n], ACT.Exp, scale=1.0 / WS).then_inc(done, 1)

            def gn(part, b):
                if part == 0:
                    wait(act, xt_free, b.value(1, 0))
                    for c in range(NC):
                        m.k += 1
                        act.wait_ge(m_full, m.value())
                        a.activation(xt[:, CH * c:CH * (c + 1)], ps_m[0:D, :], ACT.Copy).then_inc(m_free, 1)
                if part in (1, 2):
                    m.k += 1
                if part == 3:
                    m.k += 1
                    exponentials(ra, sub_a, exp_a, EA, b)
                if part == 4:
                    m.k += 1
                if part == 5:
                    m.k += 2

            def x_load(b):
                wait(act, acc_ready, b.value(1, 0))
                act.dma_start(xin[:], x_d[b.value(1, 0)]).then_inc(x_loaded, 16)

            def store(b):
                act.wait_ge(xo_ready, b.value(1, 1))
                act.dma_start(out_d[b.value(1, 0)], xo[:]).then_inc(out_done, 16)

            def softmax(b):
                for n, (t, c, j) in enumerate(SOFT_STEPS):
                    w = CH * (c + 1) - max(CH * c, P * j)
                    if n < 2:
                        wait(act, pv_step, b.value(STEPS, 0))
                    else:
                        act.wait_ge(pv_step, b.value(STEPS, n - 1))
                    for g in range(TR):
                        k = n * TR + g
                        act.wait_ge(s_full, b.value(SU, k + 1))
                        a.activation(probs[:, n % 2, g, 0:w], ps_r[k % 3][:, 0:w], ACT.Exp,
                                     scale=float(HD) ** -0.5).then_inc(p_ready, 1)

            def iteration(it, moe_a, attend, moe_c):
                def in_a(g):
                    b1, b2 = Image(it, -1), Image(it, -2)
                    if g == 0 and attend:
                        m.k += 2
                    if g == 1 and attend:
                        m.k += 4
                    if g == 2 and attend:
                        wait(act, pv_step, b1.value(STEPS, 0))
                        for c in range(NC):
                            m.k += 1
                            act.wait_ge(m_full, m.value())
                            a.activation(vaug[:, TC * c:TC * (c + 1), :, 0:HD],
                                         ps_m[:, 0:TC * D].rearrange("p (t h d) -> p t h d", t=TC, h=H),
                                         ACT.Copy, scale=1.0 / WS)
                            act.drain().then_inc(m_free, 1)
                            act.nop().then_inc(v_ready, 1)
                    if g == 2 and moe_c:
                        m.k += 2
                    if g == 4 and attend:
                        wait(act, x2_ready, b1.value(1, 0))
                        act.wait_ge(ln1_var, b1.value(1, 1))
                        a.activation(x1r[:], x1[:], ACT.Copy).then_inc(x1r_ready, 1)
                    if g == 5 and moe_c:
                        m.k += 2
                    if g == 6 and moe_c:
                        m.k += 1
                    if g == 7 and moe_c:
                        exponentials(rc_, sub_c, exp_c, EC, b2)
                    if g == 9 and moe_c:
                        m.k += 1
                    if g == 10 and moe_c:
                        m.k += 2
                    if g == GA and attend:
                        m.k += 1

                def in_c(g):
                    if has_next(it):
                        slots = {0: 0, 2: 1, 3: 2, 6: 3}
                        if g in slots:
                            gn(slots[g], Image(it, 1))

                if has_next(it):
                    x_load(Image(it, 1))
                if moe_a:
                    moe(EA, in_a)
                else:
                    for g in range(GA + 1):
                        in_a(g)
                if moe_c:
                    moe(EC, in_c)
                else:
                    for g in range(GC + 1):
                        in_c(g)
                if has_next(it):
                    gn(4, None)
                    gn(5, None)
                if moe_c:
                    store(Image(it, -2))
                if attend:
                    softmax(Image(it, -1))

            x_load(Image(0, 0))
            m.k += M_SETUP
            for part in range(6):
                gn(part, Image(0, 0))
            walk(act, [m, grp], iteration)
            act.wait_ge(out_done, 16 * NIMG)

        @block.vector
        def _(dve):
            m, grp = Count(M_ITER), Count(GA + GC)
            v = nc.vector

            def split(hi, lo, src, scale):
                v.tensor_scalar(hi, src, scale, None, ALU.mult)
                dve.drain()
                return v.scalar_tensor_tensor(out=lo, in0=src, scalar=scale, in1=hi, op0=ALU.mult,
                                              op1=ALU.subtract)

            def shared():
                m.k += 1
                dve.wait_ge(m_full, m.value())

            def split_turned(xh, xl, ready):
                for c in range(NC):
                    shared()
                    tok = slice(CH * c, CH * (c + 1))
                    split(xh[0:D, tok], xl[0:D, tok], ps_m[0:D, :], 1.0).then_inc(m_free, 1)
                dve.drain().then_inc(ready, 1)

            def top_two(r, values):
                for t in range(TT):
                    v.max(r.top[:, t, :], values[:, t, :])
                dve.drain()
                for t in range(TT):
                    v.max_index(r.idx[:, t, :], r.top[:, t, :], values[:, t, :])
                dve.drain()
                for dst, n in ((r.first, 0), (r.second, 1)):
                    v.tensor_tensor(dst[:], expert[:], r.idx[:, :, n:n + 1].to_broadcast([P, TT, 8]), ALU.is_equal)
                dve.drain()
                v.tensor_tensor(r.first[:], r.first[:], r.second[:], ALU.add)

            def scores(r, n, ready):
                shared()
                v.tensor_copy(r.score[:, :, 0:n],
                              ps_m[:, 0:TT * 8].rearrange("p (t e) -> p t e", e=8)[:, :, 0:n]).then_inc(m_free, 1)
                dve.drain()
                v.tensor_reduce(r.total[:], r.score[:, :, 0:n], AX, ALU.max)
                dve.drain()
                v.tensor_tensor(r.shifted[:, :, 0:n], r.score[:, :, 0:n],
                                r.total[:].unsqueeze(2).to_broadcast([P, TT, n]), ALU.subtract).then_inc(ready, 1)

            def normalise(r, dst, src, n, eps):
                v.tensor_reduce(r.total[:], src, AX, ALU.add)
                dve.drain()
                if eps:
                    v.tensor_scalar(r.total[:], r.total[:], eps, None, ALU.add)
                    dve.drain()
                v.reciprocal(r.inv[:], r.total[:])
                dve.drain()
                return v.tensor_tensor(dst, src, r.inv[:].unsqueeze(2).to_broadcast([P, TT, n]), ALU.mult)

            def gates_out(r, done, b):
                shared()
                v.tensor_copy(r.gt[:], ps_m[:, 0:P]).then_inc(m_free, 1)
                dve.drain().then_inc(done, 1)

            def gn(part, b):
                if part == 0:
                    m.k += 2
                    dve.wait_ge(m_free, m.value())
                    for c in range(NC):
                        v.bn_stats(gst[:, c, :], xt[:, CH * c:CH * (c + 1)])
                    dve.drain()
                    v.bn_aggr(gmv[:], gst[:]).then_inc(gn_in, 1)
                if part == 1:
                    shared()
                    v.tensor_copy(gmean[:], ps_m[0:D, 0:1]).then_inc(m_free, 1)
                    dve.drain()
                    v.tensor_tensor(gdev[:], gmv[:, 0:1], gmean[:], ALU.subtract)
                    dve.drain()
                    v.scalar_tensor_tensor(out=gspread[:], in0=gdev[:], scalar=gdev[:], in1=gmv[:, 1:2],
                                           op0=ALU.mult, op1=ALU.add).then_inc(gn_in, 1)
                if part == 2:
                    shared()
                    v.tensor_copy(gvar[:], ps_m[0:D, 0:1]).then_inc(m_free, 1)
                    dve.drain().then_inc(gn_var, 1)
                    dve.wait_ge(gn_rstd, b.value(1, 1))
                    v.tensor_scalar(xt[:], xt[:], gmean[:], grstd[:], ALU.subtract, ALU.mult)
                    dve.drain()
                    v.tensor_copy(xah[0:D, :], xt[:])
                    dve.drain()
                    v.tensor_tensor(xal[0:D, :], xt[:], xah[0:D, :], ALU.subtract).then_inc(xt_free, 1)
                if part == 3:
                    scores(ra, EA, sub_a)
                    top_two(ra, ra.score)
                    dve.drain()
                    dve.wait_ge(exp_a, b.value(1, 1))
                    v.tensor_tensor(ra.prob[:], ra.ex[:], ra.first[:], ALU.mult)
                    dve.drain()
                    normalise(ra, ra.gates[:, 0:TT, :], ra.prob[:], EA, 0.0).then_inc(gates_a, 1)
                if part == 4:
                    gates_out(ra, gt_a, b)
                if part == 5:
                    for c in range(NC):
                        shared()
                        tiles = slice(TC * c, TC * (c + 1))
                        v.tensor_tensor(acc[:, tiles, :], ps_m[:, 0:TC * D].rearrange("p (t d) -> p t d", t=TC),
                                        xin[:, tiles, :], ALU.add).then_inc(m_free, 1)
                    dve.drain().then_inc(acc_ready, 1)

            def route_c(part, b):
                if part == 0:
                    scores(rc_, EC, sub_c)
                if part == 1:
                    dve.wait_ge(exp_c, b.value(1, 1))
                    normalise(rc_, rc_.prob[:, :, 0:EC], rc_.ex[:, :, 0:EC], EC, 0.0)
                    dve.drain()
                    top_two(rc_, rc_.prob)
                    dve.drain()
                    v.tensor_tensor(rc_.ex[:, :, 0:EC], rc_.prob[:, :, 0:EC], rc_.first[:, :, 0:EC], ALU.mult)
                    dve.drain()
                    normalise(rc_, rc_.gates[:, 0:TT, 0:EC], rc_.ex[:, :, 0:EC], EC, 1e-9).then_inc(gates_c, 1)

            def combine(r, e, c, ring, src, dst, last):
                bank = ring[grp.k % 2]
                dve.wait_ge(y_full, grp.value(1, 1))
                for i in range(TC):
                    t = TC * c + i
                    last = v.scalar_tensor_tensor(out=dst[:, t, :], in0=bank[:, D * i:D * (i + 1)],
                                                  scalar=r.gates[:, t, e:e + 1], in1=src[:, t, :],
                                                  op0=ALU.mult, op1=ALU.add)
                last.then_inc(y_free, 1)
                grp.k += 1

            def moe(r, ne, src, final, before_final, between):
                for g in range(NC * ne + 1):
                    if g > 0:
                        c, e = (g - 1) // ne, (g - 1) % ne
                        if e == ne - 1 and c == 0:
                            before_final()
                        wait(dve, y_free, grp.value())
                        combine(r, e, c, ps_y, src, final if e == ne - 1 else src, None)
                    between(g)

            def ln_stats(src, mv, ready):
                for t in range(TT):
                    v.bn_stats(st[:, t, :], src[:, t, :])
                dve.drain()
                for t in range(TT):
                    v.bn_aggr(mv[:, t, :], st[:, t, :])
                dve.drain().then_inc(ready, 1)

            def ln_apply(dst, src, mv, rstd, got, ready, b):
                dve.wait_ge(got, b.value(1, 1))
                for t in range(TT):
                    v.tensor_scalar(dst[:, t, :], src[:, t, :], mv[:, t, 0:1], rstd[:, t:t + 1],
                                    ALU.subtract, ALU.mult)
                dve.drain().then_inc(ready, 1)

            def split_qk(b):
                wait(dve, qk_stacked, b.value(16 * QK_DMAS, 0))
                for s in range(2):
                    for c in range(NC):
                        shared()
                        tok = slice(CH * c, CH * (c + 1))
                        split(qk_h[:, s, tok], qk_l[:, s, tok], ps_m[0:D, :], 1.0 / WS).then_inc(m_free, 1)
                dve.drain().then_inc(qk_split, 1)

            def maximum(b, k):
                h, i, part = MAX_UNITS[k]
                w = min(CH, P * (i + 1) - CH * part)
                dve.wait_ge(mx_full, b.value(MAXU, k + 1))
                v.tensor_reduce(mpart[:, h, i, part:part + 1], ps_r[k % 3][:, 0:w], AX, ALU.max
                                ).then_inc(mx_free, 1)

            def maxima(b):
                dve.drain()
                used = mneg[:, 0:H * TT]
                v.tensor_reduce(used.rearrange("p (h i) -> p h i", h=H), mpart[:], AX, ALU.max)
                dve.drain()
                v.tensor_scalar(used, used, -1.0 / MS, None, ALU.mult).then_inc(mneg_ready, 1)
                wait(dve, m_stacked, b.value(32, 0))
                shared()
                split(mth[:], mtl[:], ps_m[0:H * TT, 0:P], 1.0).then_inc(m_free, 1)
                dve.drain().then_inc(m_split, 1)

            def gather_values(b):
                n = 0
                for t in range(2):
                    for c in range(NC):
                        n += TC * (c + 1)
                        dve.wait_ge(pv_step, b.value(STEPS, n))
                        v.tensor_copy(yt[:, t, CH * c:CH * (c + 1)], ps_y[(2 * t + c) % 2][0:D, :]
                                      ).then_inc(pv_free, 1)
                dve.drain().then_inc(yt_ready, 1)
                wait(dve, rsum_out, b.value(16, 0))
                dve.wait_ge(sums_in, b.value(16 * H, 16 * H))
                v.reciprocal(rsum[:], sums[:]).then_inc(rsum_ready, 1)

            def iteration(it, moe_a, attend, moe_c):
                b0, b1, b2 = Image(it, 0), Image(it, -1), Image(it, -2)

                def in_a(g):
                    if g == 0 and attend:
                        wait(dve, v_ready, b1.value(NC, 0))
                        split_turned(xbh, xbl, xb_ready)
                    if g == 1 and attend:
                        split_qk(b1)
                    if g == 1 and moe_c:
                        dve.wait_ge(rb_in, b2.value(16 * H, 16 * H))
                        v.tensor_tensor(yt[:], yt[:], rb[:], ALU.mult).then_inc(yn_ready, 1)
                    if g == 2 and attend:
                        m.k += 2
                    if g == 2 and moe_c:
                        dve.wait_ge(x1r_ready, b2.value(1, 1))
                        for c in range(NC):
                            shared()
                            tiles = slice(TC * c, TC * (c + 1))
                            v.tensor_tensor(x2[:, tiles, :], ps_m[:, 0:TC * D].rearrange("p (t d) -> p t d", t=TC),
                                            x1r[:, tiles, :], ALU.add).then_inc(m_free, 1)
                        dve.drain().then_inc(x2_ready, 1)
                        ln_stats(x2, mv2, ln2_var)
                    if g == 4 and moe_c:
                        ln_apply(xn2, x2, mv2, rstd2, ln2_rstd, xn2_ready, b2)
                    if g == 5 and moe_c:
                        split_turned(xch, xcl, xc_ready)
                    if g == 6 and moe_c:
                        route_c(0, b2)
                    if g == 8 and moe_c:
                        route_c(1, b2)
                    if g == 9 and moe_c:
                        gates_out(rc_, gt_c, b2)
                    if g == 10 and moe_c:
                        for c in range(NC):
                            shared()
                            tiles = slice(TC * c, TC * (c + 1))
                            v.tensor_tensor(x2[:, tiles, :], ps_m[:, 0:TC * D].rearrange("p (t d) -> p t d", t=TC),
                                            x2[:, tiles, :], ALU.add).then_inc(m_free, 1)
                        dve.drain()
                    if attend:
                        for k in front_slots(g):
                            maximum(b1, k)
                    if g == GA and attend:
                        maxima(b1)

                def in_c(g):
                    if g == 0 and moe_a:
                        ln_stats(x1, mv1, ln1_var)
                    if has_next(it):
                        slots = {0: 0, 2: 1, 3: 2, 6: 3}
                        if g in slots:
                            gn(slots[g], Image(it, 1))
                    if g == 4 and moe_a:
                        ln_apply(xn1, x1, mv1, rstd1, ln1_rstd, xn1_ready, b0)

                def x1_free():
                    wait(dve, x1r_ready, b0.value(1, 0))

                def xo_free():
                    wait(dve, out_done, b2.value(16, 0))

                if moe_a:
                    moe(ra, EA, acc, x1, x1_free, in_a)
                    dve.wait_ge(y_free, grp.value())
                else:
                    for g in range(GA + 1):
                        in_a(g)
                if moe_c:
                    moe(rc_, EC, x2, xo, xo_free, in_c)
                    dve.drain().then_inc(xo_ready, 1)
                else:
                    for g in range(GC + 1):
                        in_c(g)
                if has_next(it):
                    gn(4, Image(it, 1))
                    gn(5, Image(it, 1))
                if attend:
                    gather_values(b1)

            dve.wait_ge(zeroed, 1)
            dve.wait_ge(consts, 1)
            dve.wait_ge(w_loaded[5], 32)
            for s in range(3):
                shared()
                w = slice(D * s, D * (s + 1))
                split(wqh[0:D, w], wql[0:D, w], ps_m[0:D, 0:D], WS).then_inc(m_free, 1)
            split(wqh[ONE:ONE + 1, :], wql[ONE:ONE + 1, :], batt[ONE:ONE + 1, :], WS)
            for t in range(2):
                shared()
                v.tensor_copy(wp[:, t, :], ps_m[0:D, 0:D]).then_inc(m_free, 1)
            dve.wait_ge(w_loaded[0], 64)
            split(wgh[:], wgl[:], wg_raw[:], WS)
            dve.wait_ge(w_loaded[1], 64)
            split(w1h[:], w1l[:], w1_raw[:], WS)
            dve.drain().then_inc(w_ready, 1)
            for part in range(6):
                gn(part, Image(0, 0))
            walk(dve, [m, grp], iteration)


_INS = ['x', 'L0_conv_Wg', 'L0_conv_bg', 'L0_conv_W1', 'L0_conv_b1', 'L0_conv_W2', 'L0_conv_b2',
        'L1_attn_w_attn', 'L1_attn_b_attn', 'L1_attn_w_proj', 'L1_attn_b_proj',
        'L1_ffn_gate_w', 'L1_ffn_gate_b', 'L1_ffn_w1', 'L1_ffn_b1', 'L1_ffn_w2', 'L1_ffn_b2']


def kernel(**inputs):
    import numpy as _np
    import concourse.bacc as _bacc
    from concourse import mybir as _mybir
    from concourse.bass_utils import run_bass_kernel_spmd as _run

    nc = _bacc.Bacc("TRN2", target_bir_lowering=False, num_devices=1)
    arrays, args = {}, []
    for name in _INS:
        a = _np.ascontiguousarray(inputs[name])
        arrays[f"in_{name}_dram"] = a
        args.append(nc.dram_tensor(f"in_{name}_dram", a.shape, _mybir.dt.from_np(a.dtype), kind="ExternalInput").ap())
    args.append(nc.dram_tensor("out_dram", (NIMG, 32, 32, D), _mybir.dt.float32, kind="ExternalOutput").ap())
    build(nc, *args)
    r = _run(nc, [arrays], core_ids=[0])
    return r.results[0]["out_dram"]
```

```python
from contextlib import ExitStack

import concourse.bass as bass
from concourse import mybir

F32 = mybir.dt.float32
F16 = mybir.dt.float16
BF16 = mybir.dt.bfloat16
I32 = mybir.dt.int32
U32 = mybir.dt.uint32
ALU = mybir.AluOpType
ACT = mybir.ActivationFunctionType
AX = mybir.AxisListType.X

P = 128
NIMG, T, D = 8, 1024, 96
TT = T // P
CH = 512
NC = T // CH
TC = CH // P
HID = 384
HT = HID // P
EA, EC = 8, 4
NE = EA + EC
H, HD = 6, 16
TR = 3
ONE = D
WS = 64.0
MS = 256.0
MROW = 96
NEG = -1.0e30
GA, GC = NC * EA, NC * EC
MAXU = H * (TC + 2 * TC)
W1_PARTS = NE // 2
STEPS = 2 * (TC + 2 * TC)
SU = STEPS * TR
FIRST_LOOP, END_LOOP = 3, NIMG - 1
SOFT_BANKS = 5
SLOTS_A, SLOTS_C = TC * (GA + 1), TC * (GC + 1)


class Count:

    def __init__(self, per):
        self.per, self.it, self.k = per, None, 0

    def enter(self, it):
        self.at_entry = self.k
        self.it, self.k = it, self.k - FIRST_LOOP * self.per

    def leave(self):
        n = self.k + FIRST_LOOP * self.per - self.at_entry
        assert n == self.per, (n, self.per)
        self.it, self.k = None, self.at_entry + (END_LOOP - FIRST_LOOP) * self.per

    def value(self, times=1, plus=0):
        k = self.k * times + plus
        return k if self.it is None else self.it * (self.per * times) + k


class Image:

    def __init__(self, it, off):
        self.it, self.off = it, off

    def value(self, per, k):
        return self.it * per + (self.off * per + k)


def wait(eng, sem, value):
    if not isinstance(value, int) or value > 0:
        eng.wait_ge(sem, value)


def walk(eng, counts, iteration):
    for it in range(FIRST_LOOP):
        iteration(it, True, it >= 1, it >= 2)
    with eng.Fori(FIRST_LOOP, END_LOOP) as it:
        for c in counts:
            c.enter(it)
        iteration(it, True, True, True)
    for c in counts:
        c.leave()
    iteration(NIMG - 1, True, True, True)
    iteration(NIMG, False, True, True)
    iteration(NIMG + 1, False, False, True)


def spread(n, slots):
    slots = list(slots)
    return {s: range(n * i // len(slots), n * (i + 1) // len(slots)) for i, s in enumerate(slots)}


CHORES = {
    "x_load":       (1, 0),
    "x_turn":       (1, 1),
    "gn_stats":     (1, 0),
    "gn_mean":      (1, 1),
    "gn_spread":    (1, 1),
    "gn_apply":     (1, 0),
    "logits_a":     (1, 1),
    "exp_a":        (1, 0),
    "route_a":      (1, 0),
    "gates_a":      (1, 1),
    "bias_a":       (1, 1),
    "ln1":          (0, 0),
    "ln1_apply":    (0, 0),
    "x1_turn":      (-1, 1),
    "qk":           (-1, 1),
    "val":          (-1, 1),
    "keep_x1":      (-1, 0),
    "max":          (-1, 0),
    "maxima":       (-1, 1),
    "sum_inverse":  (-2, 0),
    "normalise_y":  (-2, 0),
    "project":      (-2, 1),
    "ln2":          (-2, 0),
    "ln2_apply":    (-2, 0),
    "x2_turn":      (-2, 1),
    "logits_c":     (-2, 1),
    "exp_c":        (-2, 0),
    "route_c":      (-2, 0),
    "gates_c":      (-2, 1),
    "bias_c":       (-2, 1),
    "store":        (-2, 0),
    "split_gate":   (None, 0),
    "split_w1":     (None, 0),
    "turn_watt":    (None, 1),
    "turn_wp":      (None, 1),
}


def placed(*items):
    at = {}
    for slot, chore, unit, *off in items:
        at.setdefault(slot, []).append((chore, unit, off[0] if off else CHORES[chore][0]))
    return at


def maxima_at(first, last, n0, n1):
    return [(slot, "max", n0 + k) for slot, ks in spread(n1 - n0, range(first, last + 1)).items() for k in ks]


FRONT = [(0, "x1_turn", 0), (1, "x1_turn", 1), (3, "qk", 0), (5, "qk", 1), (7, "qk", 2), (9, "qk", 3),
         (11, "val", 0), (13, "val", 1)]
TO_X2 = [(10, "sum_inverse", 0), (17, "normalise_y", 0), (18, "project", 0), (20, "project", 1), (21, "ln2", 0)]
KEEP = [(22, "keep_x1", 0)]
TO_C = [(27, "ln2_apply", 0), (28, "x2_turn", 0), (30, "x2_turn", 1), (33, "logits_c", 0), (36, "exp_c", 0),
        (39, "route_c", 0), (47, "gates_c", 0), (49, "bias_c", 0), (51, "bias_c", 1)]
GN_EARLY = [(30, "x_turn", 0), (32, "x_turn", 1), (34, "gn_stats", 0), (36, "gn_mean", 0), (40, "gn_spread", 0)]
GN_LATE = [(0, "gn_apply", 0), (1, "ln1", 0), (2, "logits_a", 0), (4, "ln1_apply", 0)]
SOFT = placed((0, "exp_a", 0), (1, "route_a", 0), (4, "store", 0), (10, "gates_a", 0), (12, "bias_a", 0),
              (14, "bias_a", 1))
MAX_A = 44


def schedule(it):
    if isinstance(it, int) and it == 0:
        first = [(1, "route_a", 0, 0), (1, "split_w1", 1), (2, "split_w1", 2), (3, "split_w1", 3),
                 (5, "gates_a", 0, 0), (6, "bias_a", 0, 0), (7, "bias_a", 1, 0), (9, "x_load", 0),
                 (12, "split_w1", 4), (16, "split_w1", 5)]
        first += [(18 + n, "turn_watt", n) for n in range(3)] + [(22 + n, "turn_wp", n) for n in range(2)]
        return placed(*first, *GN_EARLY), placed(*GN_LATE), SOFT
    if isinstance(it, int) and it == 1:
        return (placed((1, "x_load", 0), *FRONT, *KEEP, *maxima_at(26, SLOTS_A - 1, 0, MAXU), *GN_EARLY),
                placed(*GN_LATE, (3, "maxima", 0)), SOFT)
    if isinstance(it, int) and it == NIMG:
        chain = [(s, c, u) for s, c, u in TO_C if c in ("ln2_apply", "x2_turn", "logits_c", "exp_c")]
        routed = [(1, "route_c", 0), (5, "gates_c", 0), (6, "bias_c", 0), (7, "bias_c", 1)]
        return (placed(*FRONT, *TO_X2, *KEEP, *chain, *maxima_at(22, 40, 0, 12)),
                placed(*routed, *maxima_at(0, SLOTS_C - 1, 12, MAXU), (SLOTS_C - 1, "maxima", 0)), SOFT)
    if isinstance(it, int) and it == NIMG + 1:
        chain = [(s, c, u) for s, c, u in TO_C if c in ("ln2_apply", "x2_turn", "logits_c", "exp_c")]
        return (placed(*TO_X2, *chain),
                placed((1, "route_c", 0), (5, "gates_c", 0), (6, "bias_c", 0), (7, "bias_c", 1)), SOFT)
    beside_c = [(0, "ln1", 0), (1, "x_turn", 0), (3, "x_turn", 1), (5, "gn_stats", 0), (6, "gn_mean", 0),
                (7, "ln1_apply", 0), (10, "gn_spread", 0), (15, "gn_apply", 0), (20, "logits_a", 0)]
    return (placed((1, "x_load", 0), *FRONT, *TO_X2, *KEEP, *TO_C, *maxima_at(26, SLOTS_A - 1, 0, MAX_A)),
            placed(*beside_c, *maxima_at(0, 24, MAX_A, MAXU), (26, "maxima", 0)), SOFT)


PROLOGUE = ["split_gate", "x_turn", "x_turn", "gn_stats", "gn_mean", "gn_spread", "split_w1", "gn_apply", "logits_a",
            "exp_a"]


def chores(it, phase, slot):
    for name, unit, off in schedule(it)[phase].get(slot, ()):
        if off is None or not isinstance(it, int) or 0 <= it + off < NIMG:
            yield name, unit, Image(it, off or 0)


def shared_uses():
    return sum(CHORES[name][1] for phase in schedule(None) for at in phase.values() for name, _, _ in at)


def run_chores(m, chore, some):
    for name, unit, b in some:
        before = m.k
        chore(name, unit, b)
        m.k = before + CHORES[name][1]


def prologue(m, chore):
    for n, name in enumerate(PROLOGUE):
        run_chores(m, chore, [(name, n - 1 if name == "x_turn" else 0, Image(0, 0))])


MAX_UNITS = [(h, i, part) for h in range(H) for i in range(TT) for part in range(1 if i < TC else 2)]
SOFT_STEPS = [(t, c, j) for t in range(2) for c in range(NC) for j in range(TC * (c + 1))]


def build(nc, x, cWg, cbg, cW1, cb1, cW2, cb2, w_attn, b_attn, w_proj, b_proj,
          fWg, fbg, fW1, fb1, fW2, fb2, out):
    nc.disable_value_cache = True
    with ExitStack() as ctx:
        def sb(name, shape, dt=F32):
            return ctx.enter_context(nc.sbuf_tensor(name, shape, dt))

        def sem(name):
            return ctx.enter_context(nc.semaphore(name))

        w1_raw = sb("w1_raw", [ONE + 1, NE * HID])
        w1h = sb("w1h", [ONE + 1, NE * HID], F16)
        w1l = sb("w1l", [ONE + 1, NE * HID], F16)
        w2 = sb("w2", [P, NE * HT, D])
        wg_raw = sb("wg_raw", [ONE + 1, NE])
        wgh = sb("wgh", [ONE + 1, NE], F16)
        wgl = sb("wgl", [ONE + 1, NE], F16)
        b2a = sb("b2a", [P, TT, D])
        b2c = sb("b2c", [P, TT, D])
        watt = sb("watt", [D, 3, D])
        batt = sb("batt", [ONE + 1, 3 * D])
        wqh = sb("wqh", [ONE + 1, 3 * D], F16)
        wql = sb("wql", [ONE + 1, 3 * D], F16)
        wpad = sb("wpad", [D, 2, TR, 32])
        wp = sb("wp", [D, 2, D])
        ident = sb("ident", [P, P])
        identb = sb("identb", [P, P], BF16)
        mask_q = sb("mask_q", [P, P], BF16)
        mask_k = sb("mask_k", [P, P], BF16)
        group = sb("group", [D, D])
        expert = sb("expert", [P, TT, 8], I32)
        power = sb("power", [P, TT])
        epsilon = sb("epsilon", [P, TT])

        xin = sb("xin", [P, TT, D])
        xt = sb("xt", [D, T])
        gst = sb("gst", [D, NC, 6])
        gmv = sb("gmv", [D, 2])
        gmean = sb("gmean", [D, 1])
        gdev = sb("gdev", [D, 1])
        gspread = sb("gspread", [D, 1])
        gvar = sb("gvar", [D, 1])
        grstd = sb("grstd", [D, 1])
        xah = sb("xah", [ONE + 1, T], F16)
        xal = sb("xal", [ONE + 1, T], F16)
        acc = sb("acc", [P, TT, D])
        x1 = sb("x1", [P, TT, D])
        hid = sb("hid", [P, 2, HT, CH])

        class Routing:
            def __init__(self, n):
                self.score = sb(f"score{n}", [P, TT, 8])
                self.top = sb(f"top{n}", [P, TT, 8])
                self.idx = sb(f"idx{n}", [P, TT, 8], U32)
                self.shifted = sb(f"shifted{n}", [P, TT, 8])
                self.ex = sb(f"ex{n}", [P, TT, 8])
                self.prob = sb(f"prob{n}", [P, TT, 8])
                self.first = sb(f"first{n}", [P, TT, 8])
                self.second = sb(f"second{n}", [P, TT, 8])
                self.total = sb(f"total{n}", [P, TT])
                self.inv = sb(f"inv{n}", [P, TT])
                self.gates = sb(f"gates{n}", [P, 2 * TT, 8])
                self.gt = sb(f"gt{n}", [P, P])

        ra, rc_ = Routing("a"), Routing("c")

        st = sb("st", [P, TT, 6])
        mv1 = sb("mv1", [P, TT, 2])
        mv2 = sb("mv2", [P, TT, 2])
        rstd1 = sb("rstd1", [P, TT])
        rstd2 = sb("rstd2", [P, TT])
        xn1 = sb("xn1", [P, TT, D])
        xn2 = sb("xn2", [P, TT, D])
        xbh = sb("xbh", [ONE + 1, T], F16)
        xbl = sb("xbl", [ONE + 1, T], F16)
        qk_h = sb("qk_h", [D, 2, T], F16)
        qk_l = sb("qk_l", [D, 2, T], F16)
        qs = sb("qs", [MROW + 2, H, T], F16)
        ks = sb("ks", [MROW + 2, H, T], F16)
        vaug = sb("vaug", [P, TT, H, 32])
        mpart = sb("mpart", [P, H, TT, 2])
        mneg = sb("mneg", [P, P])
        mth = sb("mth", [H * TT, P], F16)
        mtl = sb("mtl", [H * TT, P], F16)
        probs = sb("probs", [P, 2, TR, CH])
        yt = sb("yt", [D, 2, T])
        sums = sb("sums", [H * TT, P])
        rsum = sb("rsum", [H * TT, P])
        rb = sb("rb", [D, 2, T])
        x1r = sb("x1r", [P, TT, D])

        x2 = sb("x2", [P, TT, D])
        xch = sb("xch", [ONE + 1, T], F16)
        xcl = sb("xcl", [ONE + 1, T], F16)
        xo = sb("xo", [P, TT, D])

        rsum_dram = nc.dram_tensor("rsum_dram", (H, T), F32, kind="Internal").ap()

        ps_u = [ctx.enter_context(nc.psum_tensor(f"ps_u{i}", [P, CH], F32)) for i in range(2)]
        ps_y = [ctx.enter_context(nc.psum_tensor(f"ps_y{i}", [P, CH], F32)) for i in range(2)]
        ps_r = [ctx.enter_context(nc.psum_tensor(f"ps_r{i}", [P, CH], F32)) for i in range(3)]
        ps_m = ctx.enter_context(nc.psum_tensor("ps_m", [P, CH], F32))

        def soft_bank(k):
            return (ps_r + ps_u)[k % SOFT_BANKS]

        w_loaded = [sem(f"w_loaded{i}") for i in range(7)]
        w1_loaded = [sem(f"w1_loaded{i}") for i in range(W1_PARTS)]
        zeroed = sem("zeroed")
        zeroed_late = sem("zeroed_late")
        consts = sem("consts")
        ident_ready = sem("ident_ready")
        wg_ready = sem("wg_ready")
        w1_ready = sem("w1_ready")
        watt_ready = sem("watt_ready")
        m_full, m_free = sem("m_full"), sem("m_free")
        up_full, h_ready = sem("up_full"), sem("h_ready")
        y_full, y_free = sem("y_full"), sem("y_free")
        mx_full, mx_free = sem("mx_full"), sem("mx_free")
        s_full, p_ready = sem("s_full"), sem("p_ready")
        pv_step = sem("pv_step")
        pv_free = sem("pv_free")
        x_loaded = sem("x_loaded")
        xt_free = sem("xt_free")
        gn_var, gn_rstd = sem("gn_var"), sem("gn_rstd")
        ln1_var, ln1_rstd = sem("ln1_var"), sem("ln1_rstd")
        ln2_var, ln2_rstd = sem("ln2_var"), sem("ln2_rstd")
        gn_in = sem("gn_in")
        xn1_ready, xn2_ready = sem("xn1_ready"), sem("xn2_ready")
        xb_ready, xc_ready = sem("xb_ready"), sem("xc_ready")
        sub_a, exp_a, gates_a, gt_a = sem("sub_a"), sem("exp_a"), sem("gates_a"), sem("gt_a")
        sub_c, exp_c, gates_c, gt_c = sem("sub_c"), sem("exp_c"), sem("gates_c"), sem("gt_c")
        acc_ready = sem("acc_ready")
        qk_split, qk_stacked, v_ready = sem("qk_split"), sem("qk_stacked"), sem("v_ready")
        mneg_ready, m_split, m_stacked = sem("mneg_ready"), sem("m_split"), sem("m_stacked")
        yt_ready, sums_in, rsum_ready = sem("yt_ready"), sem("sums_in"), sem("rsum_ready")
        rsum_out, rb_in, yn_ready = sem("rsum_out"), sem("rb_in"), sem("yn_ready")
        x2_ready, x1r_ready = sem("x2_ready"), sem("x1r_ready")
        xo_ready, out_done = sem("xo_ready"), sem("out_done")

        QK_DMAS = 2 * 3 * H

        x_d = x.rearrange("b (t q) w c -> b (q w) t c", t=TT)
        out_d = out.rearrange("b (t q) w c -> b (q w) t c", t=TT)

        block = ctx.enter_context(nc.Block())

        @block.sync
        def _(sp):
            sp.dma_start(wg_raw[0:D, 0:EA], cWg).then_inc(w_loaded[0], 16)
            sp.dma_start(wg_raw[D:D + 1, 0:EA], cbg.rearrange("(a e) -> a e", a=1)).then_inc(w_loaded[0], 16)
            sp.dma_start(wg_raw[0:D, EA:NE], fWg).then_inc(w_loaded[0], 16)
            sp.dma_start(wg_raw[D:D + 1, EA:NE], fbg.rearrange("(a e) -> a e", a=1)).then_inc(w_loaded[0], 16)
            raw = w1_raw[:].rearrange("d (e f) -> d e f", e=NE)

            def load_w1(part):
                e = 2 * part
                w, b, e0 = (cW1, cb1, e) if e < EA else (fW1, fb1, e - EA)
                sp.dma_start(raw[0:D, e:e + 2, :], w[e0:e0 + 2].rearrange("e d f -> d e f")
                             ).then_inc(w1_loaded[part], 16)
                sp.dma_start(raw[D:D + 1, e:e + 2, :], b[e0:e0 + 2].rearrange("(a e) f -> a e f", a=1)
                             ).then_inc(w1_loaded[part], 16)

            load_w1(0)
            sp.dma_start(w2[:, 0:EA * HT, :], cW2.rearrange("e (j p) o -> p (e j) o", p=P)).then_inc(w_loaded[3], 16)
            load_w1(1)
            sp.wait_ge(zeroed, 1)
            for t in range(TT):
                sp.dma_start(b2a[8 * t:8 * t + EA, t, :], cb2).then_inc(w_loaded[2], 16)
            for part in range(2, W1_PARTS):
                load_w1(part)
            sp.dma_start(watt[:], w_attn.rearrange("(s o) i -> o s i", s=3)).then_inc(w_loaded[5], 16)
            sp.dma_start(batt[D:D + 1, :], b_attn.rearrange("(a o) -> a o", a=1)).then_inc(w_loaded[5], 16)
            for t in range(2):
                sp.dma_start(wpad[:, t, :, 0:HD],
                             w_proj[:, t * TR * HD:(t + 1) * TR * HD].rearrange("o (g d) -> o g d", g=TR)
                             ).then_inc(w_loaded[6], 16)
            sp.dma_start(wpad[:, 0, 0, HD:HD + 1], b_proj.rearrange("(o a) -> o a", a=1)).then_inc(w_loaded[6], 16)
            for t in range(TT):
                sp.dma_start(b2c[8 * t:8 * t + EC, t, :], fb2).then_inc(w_loaded[1], 16)
            sp.dma_start(w2[:, EA * HT:, :], fW2.rearrange("e (j p) o -> p (e j) o", p=P)).then_inc(w_loaded[4], 16)
            sp.wait_ge(zeroed_late, 1)

            def stack_qk(s, b):
                if s == 0:
                    wait(sp, s_full, b.value(SU, 0))
                wait(sp, qk_split, b.value(2, s + 1))
                dst, parts = ((qs, (qk_h, qk_l, qk_h)), (ks, (qk_h, qk_h, qk_l)))[s]
                for n, part in enumerate(parts):
                    for h in range(H):
                        sp.dma_start(dst[HD * n:HD * (n + 1), h, :], part[HD * h:HD * (h + 1), s, :]
                                     ).then_inc(qk_stacked, 16)

            def stack_maxima(b):
                wait(sp, m_split, b.value(1, 1))
                for n, part in enumerate((mth, mtl)):
                    sp.dma_start(qs[MROW + n:MROW + n + 1, :, :].rearrange("a h (i q) -> a (h i) q", q=P),
                                 part[:]).then_inc(m_stacked, 16)

            def spread_sums(b):
                wait(sp, yt_ready, b.value(1, 1))
                for t in range(2):
                    for g in range(TR):
                        n = (t * TR + g) * TT
                        sp.dma_start(sums[n:n + TT, :], yt[32 * g + HD:32 * g + HD + 1, t, :]
                                     .rearrange("a (i q) -> a i q", q=P)).then_inc(sums_in, 16)
                wait(sp, rsum_ready, b.value(1, 1))
                sp.dma_start(rsum_dram.rearrange("h (i q) -> (h i) q", q=P), rsum[:]).then_inc(rsum_out, 16)
                wait(sp, rsum_out, b.value(16, 16))
                for t in range(2):
                    for g in range(TR):
                        h = t * TR + g
                        sp.dma_start(rb[32 * g:32 * g + 32, t, :],
                                     rsum_dram[h:h + 1, :].partition_broadcast(32)).then_inc(rb_in, 16)

            def chore(name, k, b):
                if name == "qk" and k % NC == NC - 1:
                    stack_qk(k // NC, b)
                if name == "maxima":
                    stack_maxima(b)

            def iteration(it, moe_a, attend, moe_c):
                for phase, slots in ((0, SLOTS_A), (1, SLOTS_C)):
                    for slot in range(slots):
                        for name, k, b in chores(it, phase, slot):
                            chore(name, k, b)
                if attend:
                    spread_sums(Image(it, -1))

            walk(sp, [], iteration)

        @block.gpsimd
        def _(pool):
            g = nc.gpsimd
            g.memset(ident[:], 0.0)
            pool.drain()
            g.affine_select(out=ident[:], in_=ident[:], compare_op=ALU.not_equal, fill=1.0, base=0,
                            pattern=[[-1, P]], channel_multiplier=1)
            pool.drain().then_inc(ident_ready, 1)
            g.memset(group[:], 1.0 / 3.0)
            g.iota(expert[:], pattern=[[0, TT], [1, 8]], base=0, channel_multiplier=0)
            for tile, value in ((epsilon, 1e-5), (power, -0.5), (ra.gates, 0.0), (rc_.gates, 0.0),
                                (rc_.prob, -1.0), (b2a, 0.0), (b2c, 0.0), (wpad, 0.0)):
                g.memset(tile[:], value)
            pool.drain()
            for tile, value in ((xah, 1.0), (xal, 0.0), (xbh, 1.0), (xbl, 0.0), (xch, 1.0), (xcl, 0.0)):
                g.memset(tile[ONE:ONE + 1, :], value)
            pool.drain()
            grouped = group[:].rearrange("p (a r) -> p a r", r=3)
            g.affine_select(out=grouped, in_=grouped, compare_op=ALU.is_ge, fill=0.0, base=0,
                            pattern=[[-3, D // 3], [0, 3]], channel_multiplier=1)
            pool.drain()
            g.affine_select(out=grouped, in_=grouped, compare_op=ALU.is_ge, fill=0.0, base=2,
                            pattern=[[3, D // 3], [0, 3]], channel_multiplier=-1)
            pool.drain().then_inc(zeroed, 1)

            def zero_late():
                for tile, value in ((identb, 0.0), (mask_q, 0.0), (mask_k, 0.0), (mpart, NEG), (mneg, 0.0),
                                    (vaug, 0.0), (qs, 0.0), (ks, 0.0)):
                    g.memset(tile[:], value)
                pool.drain()
                g.affine_select(out=identb[:], in_=identb[:], compare_op=ALU.not_equal, fill=1.0, base=0,
                                pattern=[[-1, P]], channel_multiplier=1)
                g.affine_select(out=mask_q[:], in_=mask_q[:], compare_op=ALU.is_ge, fill=NEG, base=0,
                                pattern=[[-1, P]], channel_multiplier=1)
                g.affine_select(out=mask_k[:], in_=mask_k[:], compare_op=ALU.is_ge, fill=NEG, base=0,
                                pattern=[[1, P]], channel_multiplier=-1)
                g.memset(vaug[:, :, :, HD:HD + 1], 1.0)
                pool.drain()
                g.memset(ks[MROW:MROW + 2, :, :], MS)
                pool.drain().then_inc(zeroed_late, 1)

            def rstd(dst, var, ready, done, b):
                pool.wait_ge(ready, b.value(1, 1))
                n = var.shape[0]
                g.tensor_tensor(dst, var, epsilon[0:n, 0:dst.shape[1]], ALU.add)
                pool.drain()
                g.tensor_tensor(dst, dst, power[0:n, 0:dst.shape[1]], ALU.pow).then_inc(done, 1)

            def chore(name, k, b):
                if name == "gn_spread":
                    rstd(grstd[:], gvar[:], gn_var, gn_rstd, b)
                if name == "ln1":
                    rstd(rstd1[:], mv1[:, :, 1], ln1_var, ln1_rstd, b)
                if name == "ln2":
                    rstd(rstd2[:], mv2[:, :, 1], ln2_var, ln2_rstd, b)

            def iteration(it, moe_a, attend, moe_c):
                for phase, slots in ((0, SLOTS_A), (1, SLOTS_C), (2, STEPS + 1)):
                    for slot in range(slots):
                        for name, k, b in chores(it, phase, slot):
                            chore(name, k, b)

            for name in PROLOGUE:
                chore(name, 0, Image(0, 0))
            zero_late()
            walk(pool, [], iteration)

        @block.tensor
        def _(pe):
            m, grp = Count(shared_uses()), Count(GA + GC)

            def mm(dst, lhsT, rhs, start=True, stop=True):
                return nc.tensor.matmul(dst, lhsT, rhs, start=start, stop=stop, skip_group_check=True)

            def split(dst, wh, wl, xh, xl, moving_x):
                pairs = ((wh, xh), (wl, xh), (wh, xl))
                for n, (w, v) in enumerate(pairs):
                    a, b = (w, v) if moving_x else (v, w)
                    last = mm(dst, a, b, n == 0, n == 2)
                return last

            def shared():
                wait(pe, m_free, m.value())
                m.k += 1

            def turn(src, c):
                shared()
                for i in range(TC):
                    last = nc.tensor.transpose(ps_m[0:D, P * i:P * (i + 1)], src[:, TC * c + i, :], ident[:])
                last.then_inc(m_full, 1)

            def logits(xh, xl, e0, n):
                shared()
                for t in range(TT):
                    tok = slice(P * t, P * (t + 1))
                    last = split(ps_m[:, 8 * t:8 * t + n], wgh[:, e0:e0 + n], wgl[:, e0:e0 + n],
                                 xh[:, tok], xl[:, tok], False)
                last.then_inc(m_full, 1)

            def gates_turn(r, ready, b):
                pe.wait_ge(ready, b.value(1, 1))
                shared()
                nc.tensor.transpose(ps_m[:, 0:P], r.gates[:].rearrange("p t e -> p (t e)"), ident[:]
                                    ).then_inc(m_full, 1)

            def bias2(r, b2, ready, b, c):
                pe.wait_ge(ready, b.value(1, 1))
                shared()
                mm(ps_m[:, 0:TC * D], r.gt[:],
                   b2[:, TC * c:TC * (c + 1), :].rearrange("p t d -> p (t d)")).then_inc(m_full, 1)

            def group_mean(part, b):
                pe.wait_ge(gn_in, b.value(2, part))
                shared()
                mm(ps_m[0:D, 0:1], group[:], gmv[:, 0:1] if part == 1 else gspread[:]).then_inc(m_full, 1)

            def up(xh, xl, e, c, j):
                wait(pe, h_ready, grp.value(HT, j - 1))
                w = slice((e * HT + j) * P, (e * HT + j + 1) * P)
                tok = slice(CH * c, CH * (c + 1))
                bank = ps_u[(HT * grp.k + j) % 2]
                split(bank[:], w1h[:, w], w1l[:, w], xh[:, tok], xl[:, tok], True).then_inc(up_full, 1)

            def down(e, i):
                if i == 0:
                    pe.wait_ge(h_ready, grp.value(HT, 0))
                    wait(pe, y_free, grp.value(1, -2))
                n = grp.k - 1
                for j in range(HT):
                    last = mm(ps_y[n % 2][:, D * i:D * (i + 1)], hid[:, n % 2, j, P * i:P * (i + 1)],
                              w2[:, e * HT + j, :], j == 0, j == HT - 1)
                if i == TC - 1:
                    last.then_inc(y_full, 1)

            def moe(xh, xl, e0, ne, it, phase):
                for g in range(NC * ne + 1):
                    new = g < NC * ne
                    if new and phase == 0 and g < EA and g % 2 == 0 and isinstance(it, int) and it == 0:
                        pe.wait_ge(w1_ready, g // 2 + 1)
                    for j in range(TC):
                        if j < HT and new:
                            up(xh, xl, e0 + g % ne, g // ne, j)
                        if g > 0:
                            if g == 1 and j == 0:
                                wait(pe, pv_free, Image(it, -2).value(4, 4))
                            down(e0 + (g - 1) % ne, j)
                        run_chores(m, chore, chores(it, phase, TC * g + j))
                    if new:
                        grp.k += 1

            def qk(s, c, b):
                pe.wait_ge(xb_ready, b.value(NC, NC))
                w = slice(D * s, D * (s + 1))
                shared()
                tok = slice(CH * c, CH * (c + 1))
                split(ps_m[0:D, :], wqh[:, w], wql[:, w], xbh[:, tok], xbl[:, tok], True).then_inc(m_full, 1)

            def values(c):
                w = slice(2 * D, 3 * D)
                shared()
                for i in range(TC):
                    tok = slice(P * (TC * c + i), P * (TC * c + i + 1))
                    last = split(ps_m[:, D * i:D * (i + 1)], wqh[:, w], wql[:, w], xbh[:, tok], xbl[:, tok], False)
                last.then_inc(m_full, 1)

            def maximum(b, k):
                h, i, part = MAX_UNITS[k]
                if k == 0:
                    pe.wait_ge(qk_stacked, b.value(16 * QK_DMAS, 16 * QK_DMAS))
                    wait(pe, p_ready, b.value(SU, 0))
                wait(pe, mx_free, b.value(MAXU, k - 2))
                k0 = CH * part
                w = min(CH, P * (i + 1) - k0)
                diagonal = k0 + w == P * (i + 1)
                bank = ps_r[k % 3]
                last = mm(bank[:, 0:w], qs[0:MROW, h, P * i:P * (i + 1)], ks[0:MROW, h, k0:k0 + w],
                          True, not diagonal)
                if diagonal:
                    last = mm(bank[:, w - P:w], identb[:], mask_q[:], False, True)
                last.then_inc(mx_full, 1)

            def maxima_turn(b):
                pe.wait_ge(mneg_ready, b.value(1, 1))
                shared()
                nc.tensor.transpose(ps_m[:, 0:P], mneg[:], ident[:]).then_inc(m_full, 1)

            def soft_scores(b, n):
                t, c, j = SOFT_STEPS[n]
                q0 = max(CH * c, P * j)
                w = CH * (c + 1) - q0
                for g in range(TR):
                    k = n * TR + g
                    if n == 0 and g == 0:
                        pe.wait_ge(m_stacked, b.value(32, 32))
                        pe.wait_ge(mx_free, b.value(MAXU, MAXU))
                    if k == TR:
                        pe.wait_ge(h_ready, grp.value(HT, 0))
                    if k >= SOFT_BANKS:
                        pe.wait_ge(p_ready, b.value(SU, k - SOFT_BANKS + 1))
                    h = t * TR + g
                    diagonal = P * j >= CH * c
                    last = mm(soft_bank(k)[:, 0:w], ks[0:MROW + 2, h, P * j:P * (j + 1)],
                              qs[0:MROW + 2, h, q0:q0 + w], True, not diagonal)
                    if diagonal:
                        last = mm(soft_bank(k)[:, 0:P], identb[:], mask_k[:], False, True)
                    last.then_inc(s_full, 1)

            def soft_values(b, n):
                t, c, j = SOFT_STEPS[n]
                q0 = max(CH * c, P * j)
                w = CH * (c + 1) - q0
                off = q0 - CH * c
                pe.wait_ge(p_ready, b.value(SU, (n + 1) * TR))
                if n == 0:
                    pe.wait_ge(v_ready, b.value(NC, NC))
                if j == 0:
                    wait(pe, pv_free, b.value(4, 2 * t + c - 1))
                for g in range(TR):
                    last = mm(ps_y[(2 * t + c) % 2][32 * g:32 * g + 32, off:off + w],
                              vaug[:, j, t * TR + g, :], probs[:, n % 2, g, 0:w],
                              j == 0, j == TC * (c + 1) - 1)
                last.then_inc(pv_step, 1)

            def softmax(it, b, attend):
                wait(pe, y_free, grp.value())
                for n in range(STEPS + 1):
                    if n < STEPS and attend:
                        soft_scores(b, n)
                    if n > 0 and attend:
                        soft_values(b, n - 1)
                    run_chores(m, chore, chores(it, 2, n))

            def project(c):
                shared()
                for i in range(TC):
                    q = P * (TC * c + i)
                    for t in range(2):
                        last = mm(ps_m[:, D * i:D * (i + 1)], yt[:, t, q:q + P], wp[:, t, :], t == 0, t == 1)
                last.then_inc(m_full, 1)

            def chore(name, k, b):
                if name == "x_turn":
                    if k == 0:
                        pe.wait_ge(x_loaded, b.value(16, 16))
                    turn(xin, k)
                if name in ("gn_mean", "gn_spread"):
                    if name == "gn_mean" and isinstance(b.value(1, 0), int) and b.value(1, 0) == 0:
                        pe.wait_ge(zeroed, 1)
                    group_mean(1 if name == "gn_mean" else 2, b)
                if name == "logits_a":
                    if isinstance(b.value(1, 0), int) and b.value(1, 0) == 0:
                        pe.wait_ge(wg_ready, 1)
                    pe.wait_ge(xt_free, b.value(1, 1))
                    logits(xah, xal, 0, EA)
                if name == "gates_a":
                    gates_turn(ra, gates_a, b)
                if name == "bias_a":
                    bias2(ra, b2a, gt_a, b, k)
                if name == "x1_turn":
                    pe.wait_ge(xn1_ready, b.value(1, 1))
                    turn(xn1, k)
                if name == "qk":
                    qk(k // NC, k % NC, b)
                if name == "val":
                    values(k)
                if name == "max":
                    maximum(b, k)
                if name == "maxima":
                    maxima_turn(b)
                if name == "project":
                    pe.wait_ge(yn_ready, b.value(1, 1))
                    project(k)
                if name == "x2_turn":
                    pe.wait_ge(xn2_ready, b.value(1, 1))
                    turn(xn2, k)
                if name == "logits_c":
                    pe.wait_ge(xc_ready, b.value(NC, NC))
                    logits(xch, xcl, EA, EC)
                if name == "gates_c":
                    gates_turn(rc_, gates_c, b)
                if name == "bias_c":
                    bias2(rc_, b2c, gt_c, b, k)
                if name == "turn_watt":
                    if k == 0:
                        pe.wait_ge(w_loaded[5], 32)
                    shared()
                    nc.tensor.transpose(ps_m[0:D, 0:D], watt[:, k, :], ident[0:D, 0:D]).then_inc(m_full, 1)
                if name == "turn_wp":
                    if k == 0:
                        pe.wait_ge(w_loaded[6], 48)
                    shared()
                    nc.tensor.transpose(ps_m[0:D, 0:D], wpad[:, k, :, :].rearrange("o g d -> o (g d)"),
                                        ident[0:D, 0:D]).then_inc(m_full, 1)

            def iteration(it, moe_a, attend, moe_c):
                wait(pe, p_ready, Image(it, -2).value(SU, SU))
                if moe_a:
                    if isinstance(it, int) and it == 0:
                        pe.wait_ge(w_loaded[3], 16)
                    moe(xah, xal, 0, EA, it, 0)
                    if isinstance(it, int) and it == 0:
                        pe.wait_ge(w1_ready, W1_PARTS)
                        pe.wait_ge(w_loaded[1], 16 * TT)
                        pe.wait_ge(w_loaded[4], 16)
                        pe.wait_ge(watt_ready, 1)
                        pe.wait_ge(zeroed_late, 1)
                else:
                    for slot in range(SLOTS_A):
                        run_chores(m, chore, chores(it, 0, slot))
                if moe_c:
                    moe(xch, xcl, EA, EC, it, 1)
                else:
                    for slot in range(SLOTS_C):
                        run_chores(m, chore, chores(it, 1, slot))
                softmax(it, Image(it, -1), attend)

            pe.wait_ge(ident_ready, 1)
            prologue(m, chore)
            pe.wait_ge(w_loaded[2], 16 * TT)
            walk(pe, [m, grp], iteration)

        @block.scalar
        def _(act):
            m, grp = Count(shared_uses()), Count(GA + GC)
            a = nc.scalar

            def moe(ne, it, phase):
                for g in range(NC * ne + 1):
                    for j in range(TC):
                        if g < NC * ne and j < HT:
                            act.wait_ge(up_full, grp.value(HT, j + 1))
                            if j == 0:
                                wait(act, y_full, grp.value(1, -1))
                            a.activation(hid[:, grp.k % 2, j, :], ps_u[(HT * grp.k + j) % 2][:], ACT.Gelu,
                                         scale=1.0 / WS).then_inc(h_ready, 1)
                        run_chores(m, chore, chores(it, phase, TC * g + j))
                    if g < NC * ne:
                        grp.k += 1

            def exponentials(r, ready, done, n, b):
                act.wait_ge(ready, b.value(1, 1))
                a.activation(r.ex[:, :, 0:n], r.shifted[:, :, 0:n], ACT.Exp, scale=1.0 / WS).then_inc(done, 1)

            def x_load(b):
                wait(act, acc_ready, b.value(1, 0))
                act.dma_start(xin[:], x_d[b.value(1, 0)]).then_inc(x_loaded, 16)

            def store(b):
                act.wait_ge(xo_ready, b.value(1, 1))
                act.dma_start(out_d[b.value(1, 0)], xo[:]).then_inc(out_done, 16)

            def softmax(it, b, attend):
                for n in range(STEPS + 1):
                    if attend and n < STEPS:
                        t, c, j = SOFT_STEPS[n]
                        w = CH * (c + 1) - max(CH * c, P * j)
                        if n < 2:
                            wait(act, pv_step, b.value(STEPS, 0))
                        else:
                            act.wait_ge(pv_step, b.value(STEPS, n - 1))
                        for g in range(TR):
                            k = n * TR + g
                            act.wait_ge(s_full, b.value(SU, k + 1))
                            a.activation(probs[:, n % 2, g, 0:w], soft_bank(k)[:, 0:w], ACT.Exp,
                                         scale=float(HD) ** -0.5).then_inc(p_ready, 1)
                    run_chores(m, chore, chores(it, 2, n))

            def chore(name, k, b):
                if name == "x_load":
                    x_load(b)
                if name == "x_turn":
                    if k == 0:
                        wait(act, xt_free, b.value(1, 0))
                    m.k += 1
                    act.wait_ge(m_full, m.value())
                    a.activation(xt[:, CH * k:CH * (k + 1)], ps_m[0:D, :], ACT.Copy).then_inc(m_free, 1)
                if name == "exp_a":
                    exponentials(ra, sub_a, exp_a, EA, b)
                if name == "exp_c":
                    exponentials(rc_, sub_c, exp_c, EC, b)
                if name == "val":
                    if k == 0:
                        wait(act, pv_step, b.value(STEPS, 0))
                        if isinstance(b.value(1, 0), int) and b.value(1, 0) == 0:
                            act.wait_ge(zeroed_late, 1)
                    m.k += 1
                    act.wait_ge(m_full, m.value())
                    a.activation(vaug[:, TC * k:TC * (k + 1), :, 0:HD],
                                 ps_m[:, 0:TC * D].rearrange("p (t h d) -> p t h d", t=TC, h=H),
                                 ACT.Copy, scale=1.0 / WS)
                    act.drain().then_inc(m_free, 1)
                    act.nop().then_inc(v_ready, 1)
                if name == "keep_x1":
                    wait(act, x2_ready, b.value(1, 0))
                    act.wait_ge(ln1_var, b.value(1, 1))
                    a.activation(x1r[:], x1[:], ACT.Copy).then_inc(x1r_ready, 1)
                if name == "store":
                    store(b)

            def iteration(it, moe_a, attend, moe_c):
                for phase, on, ne, slots in ((0, moe_a, EA, SLOTS_A), (1, moe_c, EC, SLOTS_C)):
                    if on:
                        moe(ne, it, phase)
                    else:
                        for slot in range(slots):
                            run_chores(m, chore, chores(it, phase, slot))
                softmax(it, Image(it, -1), attend)

            x_load(Image(0, 0))
            prologue(m, chore)
            walk(act, [m, grp], iteration)
            act.wait_ge(out_done, 16 * NIMG)

        @block.vector
        def _(dve):
            m, grp = Count(shared_uses()), Count(GA + GC)
            v = nc.vector

            def split(hi, lo, src, scale):
                v.tensor_scalar(hi, src, scale, None, ALU.mult)
                dve.drain()
                return v.scalar_tensor_tensor(out=lo, in0=src, scalar=scale, in1=hi, op0=ALU.mult,
                                              op1=ALU.subtract)

            def shared():
                m.k += 1
                dve.wait_ge(m_full, m.value())

            def split_turned(xh, xl, c, ready):
                shared()
                tok = slice(CH * c, CH * (c + 1))
                split(xh[0:D, tok], xl[0:D, tok], ps_m[0:D, :], 1.0).then_inc(m_free, 1)
                dve.drain().then_inc(ready, 1)

            def top_two(r, values):
                for t in range(TT):
                    v.max(r.top[:, t, :], values[:, t, :])
                dve.drain()
                for t in range(TT):
                    v.max_index(r.idx[:, t, :], r.top[:, t, :], values[:, t, :])
                dve.drain()
                for dst, n in ((r.first, 0), (r.second, 1)):
                    v.tensor_tensor(dst[:], expert[:], r.idx[:, :, n:n + 1].to_broadcast([P, TT, 8]), ALU.is_equal)
                dve.drain()
                v.tensor_tensor(r.first[:], r.first[:], r.second[:], ALU.add)

            def scores(r, n, ready):
                shared()
                v.tensor_copy(r.score[:, :, 0:n],
                              ps_m[:, 0:TT * 8].rearrange("p (t e) -> p t e", e=8)[:, :, 0:n]).then_inc(m_free, 1)
                dve.drain()
                v.tensor_reduce(r.total[:], r.score[:, :, 0:n], AX, ALU.max)
                dve.drain()
                v.tensor_tensor(r.shifted[:, :, 0:n], r.score[:, :, 0:n],
                                r.total[:].unsqueeze(2).to_broadcast([P, TT, n]), ALU.subtract).then_inc(ready, 1)

            def normalise(r, dst, src, n, eps):
                v.tensor_reduce(r.total[:], src, AX, ALU.add)
                dve.drain()
                if eps:
                    v.tensor_scalar(r.total[:], r.total[:], eps, None, ALU.add)
                    dve.drain()
                v.reciprocal(r.inv[:], r.total[:])
                dve.drain()
                return v.tensor_tensor(dst, src, r.inv[:].unsqueeze(2).to_broadcast([P, TT, n]), ALU.mult)

            def gates_out(r, done, b):
                shared()
                v.tensor_copy(r.gt[:], ps_m[:, 0:P]).then_inc(m_free, 1)
                dve.drain().then_inc(done, 1)

            def combine(r, e, c, ring, src, dst, last):
                bank = ring[grp.k % 2]
                dve.wait_ge(y_full, grp.value(1, 1))
                for i in range(TC):
                    t = TC * c + i
                    last = v.scalar_tensor_tensor(out=dst[:, t, :], in0=bank[:, D * i:D * (i + 1)],
                                                  scalar=r.gates[:, t, e:e + 1], in1=src[:, t, :],
                                                  op0=ALU.mult, op1=ALU.add)
                last.then_inc(y_free, 1)
                grp.k += 1

            def moe(r, ne, src, final, before_final, it, phase):
                for g in range(NC * ne + 1):
                    for j in range(TC):
                        run_chores(m, chore, chores(it, phase, TC * g + j))
                    if g > 0:
                        c, e = (g - 1) // ne, (g - 1) % ne
                        if e == ne - 1 and c == 0:
                            before_final()
                        wait(dve, y_free, grp.value())
                        combine(r, e, c, ps_y, src, final if e == ne - 1 else src, None)

            def ln_stats(src, mv, ready):
                for t in range(TT):
                    v.bn_stats(st[:, t, :], src[:, t, :])
                dve.drain()
                for t in range(TT):
                    v.bn_aggr(mv[:, t, :], st[:, t, :])
                dve.drain().then_inc(ready, 1)

            def ln_apply(dst, src, mv, rstd, got, ready, b):
                dve.wait_ge(got, b.value(1, 1))
                for t in range(TT):
                    v.tensor_scalar(dst[:, t, :], src[:, t, :], mv[:, t, 0:1], rstd[:, t:t + 1],
                                    ALU.subtract, ALU.mult)
                dve.drain().then_inc(ready, 1)

            def split_qk(s, c, b):
                if s == 0 and c == 0:
                    wait(dve, qk_stacked, b.value(16 * QK_DMAS, 0))
                shared()
                tok = slice(CH * c, CH * (c + 1))
                split(qk_h[:, s, tok], qk_l[:, s, tok], ps_m[0:D, :], 1.0 / WS).then_inc(m_free, 1)
                if c == NC - 1:
                    dve.drain().then_inc(qk_split, 1)

            def maximum(b, k):
                h, i, part = MAX_UNITS[k]
                w = min(CH, P * (i + 1) - CH * part)
                if k == 0 and isinstance(b.value(1, 0), int) and b.value(1, 0) == 0:
                    dve.wait_ge(zeroed_late, 1)
                dve.wait_ge(mx_full, b.value(MAXU, k + 1))
                v.tensor_reduce(mpart[:, h, i, part:part + 1], ps_r[k % 3][:, 0:w], AX, ALU.max
                                ).then_inc(mx_free, 1)

            def maxima(b):
                dve.drain()
                used = mneg[:, 0:H * TT]
                v.tensor_reduce(used.rearrange("p (h i) -> p h i", h=H), mpart[:], AX, ALU.max)
                dve.drain()
                v.tensor_scalar(used, used, -1.0 / MS, None, ALU.mult).then_inc(mneg_ready, 1)
                wait(dve, m_stacked, b.value(32, 0))
                shared()
                split(mth[:], mtl[:], ps_m[0:H * TT, 0:P], 1.0).then_inc(m_free, 1)
                dve.drain().then_inc(m_split, 1)

            def softmax(it, b, attend):
                ends = {TC: 0, TC + 2 * TC: 1, TC + 3 * TC: 2, 2 * (TC + 2 * TC): 3}
                for n in range(STEPS + 1):
                    run_chores(m, chore, chores(it, 2, n))
                    if attend and n in ends:
                        t, c = ends[n] // NC, ends[n] % NC
                        dve.wait_ge(pv_step, b.value(STEPS, n))
                        v.tensor_copy(yt[:, t, CH * c:CH * (c + 1)], ps_y[ends[n] % 2][0:D, :]).then_inc(pv_free, 1)
                if attend:
                    dve.drain().then_inc(yt_ready, 1)

            def chore(name, k, b):
                tiles = slice(TC * k, TC * (k + 1))
                if name == "split_gate":
                    dve.wait_ge(w_loaded[0], 64)
                    split(wgh[:], wgl[:], wg_raw[:], WS)
                    dve.drain().then_inc(wg_ready, 1)
                if name == "split_w1":
                    dve.wait_ge(w1_loaded[k], 32)
                    w = slice(2 * HID * k, 2 * HID * (k + 1))
                    split(w1h[:, w], w1l[:, w], w1_raw[:, w], WS)
                    dve.drain().then_inc(w1_ready, 1)
                if name == "turn_watt":
                    shared()
                    w = slice(D * k, D * (k + 1))
                    split(wqh[0:D, w], wql[0:D, w], ps_m[0:D, 0:D], WS).then_inc(m_free, 1)
                    if k == 0:
                        dve.wait_ge(w_loaded[5], 32)
                        split(wqh[ONE:ONE + 1, :], wql[ONE:ONE + 1, :], batt[ONE:ONE + 1, :], WS)
                if name == "turn_wp":
                    shared()
                    v.tensor_copy(wp[:, k, :], ps_m[0:D, 0:D]).then_inc(m_free, 1)
                    if k == 1:
                        dve.drain().then_inc(watt_ready, 1)
                if name == "gn_stats":
                    dve.wait_ge(m_free, m.value())
                    for c in range(NC):
                        v.bn_stats(gst[:, c, :], xt[:, CH * c:CH * (c + 1)])
                    dve.drain()
                    v.bn_aggr(gmv[:], gst[:]).then_inc(gn_in, 1)
                if name == "gn_mean":
                    shared()
                    v.tensor_copy(gmean[:], ps_m[0:D, 0:1]).then_inc(m_free, 1)
                    dve.drain()
                    v.tensor_tensor(gdev[:], gmv[:, 0:1], gmean[:], ALU.subtract)
                    dve.drain()
                    v.scalar_tensor_tensor(out=gspread[:], in0=gdev[:], scalar=gdev[:], in1=gmv[:, 1:2],
                                           op0=ALU.mult, op1=ALU.add).then_inc(gn_in, 1)
                if name == "gn_spread":
                    shared()
                    v.tensor_copy(gvar[:], ps_m[0:D, 0:1]).then_inc(m_free, 1)
                    dve.drain().then_inc(gn_var, 1)
                if name == "gn_apply":
                    dve.wait_ge(gn_rstd, b.value(1, 1))
                    v.tensor_scalar(xt[:], xt[:], gmean[:], grstd[:], ALU.subtract, ALU.mult)
                    dve.drain()
                    v.tensor_copy(xah[0:D, :], xt[:])
                    dve.drain()
                    v.tensor_tensor(xal[0:D, :], xt[:], xah[0:D, :], ALU.subtract).then_inc(xt_free, 1)
                if name == "logits_a":
                    scores(ra, EA, sub_a)
                if name == "route_a":
                    top_two(ra, ra.score)
                    dve.drain()
                    dve.wait_ge(exp_a, b.value(1, 1))
                    v.tensor_tensor(ra.prob[:], ra.ex[:], ra.first[:], ALU.mult)
                    dve.drain()
                    normalise(ra, ra.gates[:, 0:TT, :], ra.prob[:], EA, 0.0).then_inc(gates_a, 1)
                if name == "gates_a":
                    gates_out(ra, gt_a, b)
                if name == "bias_a":
                    shared()
                    v.tensor_tensor(acc[:, tiles, :], ps_m[:, 0:TC * D].rearrange("p (t d) -> p t d", t=TC),
                                    xin[:, tiles, :], ALU.add).then_inc(m_free, 1)
                    if k == NC - 1:
                        dve.drain().then_inc(acc_ready, 1)
                if name == "ln1":
                    dve.wait_ge(y_free, grp.value())
                    ln_stats(x1, mv1, ln1_var)
                if name == "ln1_apply":
                    ln_apply(xn1, x1, mv1, rstd1, ln1_rstd, xn1_ready, b)
                if name == "x1_turn":
                    if k == 0:
                        wait(dve, v_ready, b.value(NC, 0))
                    split_turned(xbh, xbl, k, xb_ready)
                if name == "qk":
                    split_qk(k // NC, k % NC, b)
                if name == "max":
                    maximum(b, k)
                if name == "maxima":
                    maxima(b)
                if name == "sum_inverse":
                    wait(dve, rsum_out, b.value(16, 0))
                    dve.wait_ge(sums_in, b.value(16 * H, 16 * H))
                    v.reciprocal(rsum[:], sums[:]).then_inc(rsum_ready, 1)
                if name == "normalise_y":
                    dve.wait_ge(rb_in, b.value(16 * H, 16 * H))
                    v.tensor_tensor(yt[:], yt[:], rb[:], ALU.mult).then_inc(yn_ready, 1)
                if name == "project":
                    if k == 0:
                        dve.wait_ge(x1r_ready, b.value(1, 1))
                    shared()
                    v.tensor_tensor(x2[:, tiles, :], ps_m[:, 0:TC * D].rearrange("p (t d) -> p t d", t=TC),
                                    x1r[:, tiles, :], ALU.add).then_inc(m_free, 1)
                    if k == NC - 1:
                        dve.drain().then_inc(x2_ready, 1)
                if name == "ln2":
                    ln_stats(x2, mv2, ln2_var)
                if name == "ln2_apply":
                    ln_apply(xn2, x2, mv2, rstd2, ln2_rstd, xn2_ready, b)
                if name == "x2_turn":
                    split_turned(xch, xcl, k, xc_ready)
                if name == "logits_c":
                    scores(rc_, EC, sub_c)
                if name == "route_c":
                    dve.wait_ge(exp_c, b.value(1, 1))
                    normalise(rc_, rc_.prob[:, :, 0:EC], rc_.ex[:, :, 0:EC], EC, 0.0)
                    dve.drain()
                    top_two(rc_, rc_.prob)
                    dve.drain()
                    v.tensor_tensor(rc_.ex[:, :, 0:EC], rc_.prob[:, :, 0:EC], rc_.first[:, :, 0:EC], ALU.mult)
                    dve.drain()
                    normalise(rc_, rc_.gates[:, 0:TT, 0:EC], rc_.ex[:, :, 0:EC], EC, 1e-9).then_inc(gates_c, 1)
                if name == "gates_c":
                    gates_out(rc_, gt_c, b)
                if name == "bias_c":
                    shared()
                    v.tensor_tensor(x2[:, tiles, :], ps_m[:, 0:TC * D].rearrange("p (t d) -> p t d", t=TC),
                                    x2[:, tiles, :], ALU.add).then_inc(m_free, 1)
                    if k == NC - 1:
                        dve.drain()

            def iteration(it, moe_a, attend, moe_c):
                def x1_free():
                    wait(dve, x1r_ready, Image(it, 0).value(1, 0))

                def xo_free():
                    wait(dve, out_done, Image(it, -2).value(16, 0))

                if moe_a:
                    moe(ra, EA, acc, x1, x1_free, it, 0)
                else:
                    for slot in range(SLOTS_A):
                        run_chores(m, chore, chores(it, 0, slot))
                if moe_c:
                    moe(rc_, EC, x2, xo, xo_free, it, 1)
                    dve.drain().then_inc(xo_ready, 1)
                else:
                    for slot in range(SLOTS_C):
                        run_chores(m, chore, chores(it, 1, slot))
                softmax(it, Image(it, -1), attend)

            dve.wait_ge(zeroed, 1)
            prologue(m, chore)
            walk(dve, [m, grp], iteration)


_INS = ['x', 'L0_conv_Wg', 'L0_conv_bg', 'L0_conv_W1', 'L0_conv_b1', 'L0_conv_W2', 'L0_conv_b2',
        'L1_attn_w_attn', 'L1_attn_b_attn', 'L1_attn_w_proj', 'L1_attn_b_proj',
        'L1_ffn_gate_w', 'L1_ffn_gate_b', 'L1_ffn_w1', 'L1_ffn_b1', 'L1_ffn_w2', 'L1_ffn_b2']


def kernel(**inputs):
    import numpy as _np
    import concourse.bacc as _bacc
    from concourse import mybir as _mybir
    from concourse.bass_utils import run_bass_kernel_spmd as _run

    nc = _bacc.Bacc("TRN2", target_bir_lowering=False, num_devices=1)
    arrays, args = {}, []
    for name in _INS:
        a = _np.ascontiguousarray(inputs[name])
        arrays[f"in_{name}_dram"] = a
        args.append(nc.dram_tensor(f"in_{name}_dram", a.shape, _mybir.dt.from_np(a.dtype), kind="ExternalInput").ap())
    args.append(nc.dram_tensor("out_dram", (NIMG, 32, 32, D), _mybir.dt.float32, kind="ExternalOutput").ap())
    build(nc, *args)
    r = _run(nc, [arrays], core_ids=[0])
    return r.results[0]["out_dram"]
```

```python
from collections import namedtuple
from contextlib import ExitStack

import concourse.bass as bass
from concourse import mybir

F32 = mybir.dt.float32
F16 = mybir.dt.float16
BF16 = mybir.dt.bfloat16
I32 = mybir.dt.int32
U32 = mybir.dt.uint32
ALU = mybir.AluOpType
ACT = mybir.ActivationFunctionType
AX = mybir.AxisListType.X

P = 128
NIMG, T, D = 8, 1024, 96
TT = T // P
CH = 512
NC = T // CH
TC = CH // P
HID = 384
HT = HID // P
EA, EC = 8, 4
NE = EA + EC
H, HD = 6, 16
TR = 3
ONE = D
WS = 64.0
MS = 256.0
MROW = 96
NEG = -1.0e30
GA, GC = NC * EA, NC * EC
MAXU = H * (TC + 2 * TC)
W1_PARTS = NE // 2
STEPS = 2 * (TC + 2 * TC)
SU = STEPS * TR
FIRST_LOOP, END_LOOP = 3, NIMG - 1
ZEROS = 8
SLOTS_A, SLOTS_C = TC * GA, TC * (GC + 1)


class Count:

    def __init__(self, per):
        self.per, self.it, self.k = per, None, 0

    def enter(self, it):
        self.at_entry = self.k
        self.it, self.k = it, self.k - FIRST_LOOP * self.per

    def leave(self):
        n = self.k + FIRST_LOOP * self.per - self.at_entry
        assert n == self.per, (n, self.per)
        self.it, self.k = None, self.at_entry + (END_LOOP - FIRST_LOOP) * self.per

    def value(self, times=1, plus=0):
        k = self.k * times + plus
        return k if self.it is None else self.it * (self.per * times) + k


class Image:

    def __init__(self, it, off):
        self.it, self.off = it, off

    def value(self, per, k):
        return self.it * per + (self.off * per + k)


def wait(eng, sem, value):
    if not isinstance(value, int) or value > 0:
        eng.wait_ge(sem, value)


def walk(eng, counts, iteration):
    for it in range(FIRST_LOOP):
        iteration(it, True, it >= 1, it >= 2)
    with eng.Fori(FIRST_LOOP, END_LOOP) as it:
        for c in counts:
            c.enter(it)
        iteration(it, True, True, True)
    for c in counts:
        c.leave()
    iteration(NIMG - 1, True, True, True)
    iteration(NIMG, False, True, False)
    iteration(NIMG + 1, False, False, True)
    iteration(NIMG + 2, False, False, True)


def image_c(it):
    return Image(it, -3 if isinstance(it, int) and it > NIMG else -2)


def spread(n, slots):
    slots = list(slots)
    return {s: range(n * i // len(slots), n * (i + 1) // len(slots)) for i, s in enumerate(slots)}


CHORES = {
    "x_load":       (1, 0),
    "x_turn":       (1, 1),
    "gn_stats":     (1, 0),
    "gn_mean":      (1, 1),
    "gn_spread":    (1, 1),
    "gn_apply":     (1, 0),
    "logits_a":     (1, 1),
    "exp_a":        (1, 0),
    "route_a":      (1, 0),
    "gates_a":      (1, 1),
    "bias_a":       (1, 1),
    "ln1":          (0, 0),
    "ln1_apply":    (0, 0),
    "x1_turn":      (0, 1),
    "qk":           (0, 1),
    "val":          (-1, 1),
    "keep_x1":      (-1, 0),
    "max":          (-1, 0),
    "maxima":       (-1, 1),
    "sum_inverse":  (-2, 0),
    "normalise_y":  (-2, 0),
    "project":      (-2, 1),
    "ln2":          (-2, 0),
    "ln2_apply":    (-2, 0),
    "x2_turn":      (-2, 1),
    "logits_c":     (-2, 1),
    "exp_c":        (-2, 0),
    "route_c":      (-2, 0),
    "gates_c":      (-2, 1),
    "bias_c":       (-2, 1),
    "store":        (-2, 0),
    "split_gate":   (None, 0),
    "split_w1":     (None, 0),
    "split_w2":     (None, 0),
    "turn_watt":    (None, 1),
    "turn_wp":      (None, 1),
    "zero":         (None, 0),
}


def placed(*items):
    at = {}
    for slot, chore, unit, *off in items:
        at.setdefault(slot, []).append((chore, unit, off[0] if off else CHORES[chore][0]))
    return at


def maxima_at(first, last, n0, n1):
    return [(slot, "max", n0 + k) for slot, ks in spread(n1 - n0, range(first, last + 1)).items() for k in ks]


VALUES = [(0, "val", 0), (2, "val", 1)]
TO_X2 = [(4, "sum_inverse", 0), (16, "normalise_y", 0), (17, "normalise_y", 1), (19, "project", 0),
         (21, "project", 1), (22, "ln2", 0), (23, "ln2", 1)]
KEEP = [(22, "keep_x1", 0)]
TO_C = [(27, "ln2_apply", 0), (28, "ln2_apply", 1), (30, "x2_turn", 0), (32, "x2_turn", 1), (34, "logits_c", 0),
        (36, "exp_c", 0)]
ROUTE_C = [(38, "route_c", 0), (40, "route_c", 1), (42, "route_c", 2), (44, "route_c", 3), (48, "gates_c", 0)]
ROUTE_C_LATE = [(0, "route_c", 0), (0, "route_c", 1), (1, "route_c", 2), (1, "route_c", 3), (4, "gates_c", 0),
                (5, "bias_c", 0), (6, "bias_c", 1)]
GN = [(37, "x_turn", 0), (39, "x_turn", 1), (54, "gn_stats", 0), (56, "gn_mean", 0), (61, "gn_spread", 0)]
GN_LATE = [(0, "gn_apply", 0), (1, "ln1", 0), (1, "ln1", 1), (2, "logits_a", 0), (4, "ln1_apply", 0),
           (4, "ln1_apply", 1)]
FRONT = [(1, "x1_turn", 0), (3, "x1_turn", 1), (5, "qk", 0), (7, "qk", 1), (12, "qk", 2), (14, "qk", 3)]
SOFT = placed((0, "exp_a", 0), (0, "route_a", 0), (1, "route_a", 1), (2, "route_a", 2), (4, "store", 0),
              (10, "gates_a", 0), (20, "bias_a", 0), (22, "bias_a", 1), *FRONT)
MAX_A = 56


def schedule(it):
    if isinstance(it, int) and it == 0:
        first = [(0, "split_w2", 0), (1, "route_a", 0, 0), (1, "route_a", 1, 0), (1, "route_a", 2, 0),
                 (2, "split_w1", 1), (3, "gates_a", 0, 0), (4, "bias_a", 0, 0), (5, "bias_a", 1, 0),
                 (6, "split_w2", 1), (7, "x_load", 0)]
        first += [(8 + 2 * n, ("split_w1", "split_w2")[n % 2], 2 + n // 2) for n in range(2 * W1_PARTS - 4)]
        first += [(25 + n, "turn_watt", n) for n in range(3)] + [(29 + n, "turn_wp", n) for n in range(2)]
        first += [(32 + 2 * n, "zero", n) for n in range(ZEROS)]
        return placed(*first, *GN), placed((0, "gn_apply", 0)), placed()
    if isinstance(it, int) and it == 1:
        first = [(0, "logits_a", 0, 0), (0, "exp_a", 0, 0), (1, "route_a", 0, 0), (1, "route_a", 1, 0),
                 (2, "route_a", 2, 0), (4, "gates_a", 0, 0), (5, "bias_a", 0, 0), (6, "bias_a", 1, 0),
                 (7, "ln1", 0, -1), (8, "ln1", 1, -1), (8, "x_load", 0), (11, "ln1_apply", 0, -1),
                 (12, "ln1_apply", 1, -1)]
        first += [(14 + 2 * n, "x1_turn", n, -1) for n in range(NC)] + [(18 + 2 * n, "qk", n, -1) for n in range(2 * NC)]
        return (placed(*first, (26, "val", 0), (28, "val", 1), (29, "keep_x1", 0),
                       *maxima_at(32, SLOTS_A - 1, 0, MAXU), *GN),
                placed(*GN_LATE, (3, "maxima", 0)), SOFT)
    if isinstance(it, int) and it == NIMG:
        return (placed(*VALUES, (16, "sum_inverse", 0), (34, "normalise_y", 0), (35, "normalise_y", 1),
                       (37, "project", 0), (40, "project", 1), (41, "keep_x1", 0),
                       *maxima_at(3, SLOTS_A - 1, 0, MAXU)),
                placed((0, "maxima", 0)),
                placed((0, "ln2", 0), (1, "ln2", 1), (4, "ln2_apply", 0), (5, "ln2_apply", 1), (6, "x2_turn", 0),
                       (8, "x2_turn", 1), (11, "logits_c", 0), (12, "exp_c", 0), (13, "route_c", 0),
                       (14, "route_c", 1), (15, "route_c", 2), (16, "route_c", 3), (21, "gates_c", 0)))
    if isinstance(it, int) and it == NIMG + 1:
        return (placed(),
                placed((1, "bias_c", 0, -3), (4, "bias_c", 1, -3), (5, "sum_inverse", 0), (14, "normalise_y", 0),
                       (15, "normalise_y", 1), (16, "project", 0), (18, "project", 1), (19, "ln2", 0),
                       (20, "ln2", 1), (25, "ln2_apply", 0), (26, "ln2_apply", 1), (28, "x2_turn", 0),
                       (30, "x2_turn", 1)),
                placed((0, "store", 0, -3)))
    if isinstance(it, int) and it == NIMG + 2:
        return (placed(),
                placed((0, "logits_c", 0, -3), (0, "exp_c", 0, -3),
                       *((slot, name, unit, -3) for slot, name, unit in ROUTE_C_LATE)),
                placed((0, "store", 0, -3)))
    beside_c = [(1, "bias_c", 0), (4, "bias_c", 1), (5, "ln1", 0), (6, "ln1", 1), (10, "ln1_apply", 0),
                (11, "ln1_apply", 1), (13, "gn_apply", 0), (18, "logits_a", 0)]
    return (placed((1, "x_load", 0), *VALUES, *TO_X2, *KEEP, *TO_C, *ROUTE_C, *GN,
                   *maxima_at(8, SLOTS_A - 1, 0, MAX_A)),
            placed(*beside_c, *maxima_at(7, 24, MAX_A, MAXU), (26, "maxima", 0)), SOFT)


PROLOGUE = ["split_gate", "x_turn", "x_turn", "gn_stats", "gn_mean", "gn_spread", "split_w1", "gn_apply", "logits_a",
            "exp_a"]


def chores(it, phase, slot):
    for name, unit, off in schedule(it)[phase].get(slot, ()):
        if off is None or not isinstance(it, int) or 0 <= it + off < NIMG:
            yield name, unit, Image(it, off or 0)


Group = namedtuple("Group", "moe c e")


def rounds(moe_a, moe_c):
    groups = [Group(0, c, e) for c in range(NC) for e in range(EA)] * moe_a
    groups += [Group(1, c, e) for c in range(NC) for e in range(EC)] * moe_c
    if not moe_a:
        yield None, None, 0, range(SLOTS_A)
    for n, (up, down) in enumerate(zip(groups + [None], [None] + groups) if groups else ()):
        phase, g = (0, n) if moe_a and n < GA + (not moe_c) else (1, n - GA * moe_a)
        yield up, down, phase, range(TC * g, TC * (g + 1))
    if not moe_c:
        yield None, None, 1, range(SLOTS_C)


def shared_uses():
    return sum(CHORES[name][1] for phase in schedule(None) for at in phase.values() for name, _, _ in at)


def run_chores(m, chore, some):
    for name, unit, b in some:
        before = m.k
        chore(name, unit, b)
        m.k = before + CHORES[name][1]


def prologue(m, chore):
    for n, name in enumerate(PROLOGUE):
        run_chores(m, chore, [(name, n - 1 if name == "x_turn" else 0, Image(0, 0))])


MAX_UNITS = [(h, i, part) for h in range(H) for i in range(TT) for part in range(1 if i < TC else 2)]
SOFT_STEPS = [(t, c, j) for t in range(2) for c in range(NC) for j in range(TC * (c + 1))]


def build(nc, x, cWg, cbg, cW1, cb1, cW2, cb2, w_attn, b_attn, w_proj, b_proj,
          fWg, fbg, fW1, fb1, fW2, fb2, out):
    nc.disable_value_cache = True
    with ExitStack() as ctx:
        def sb(name, shape, dt=F32):
            return ctx.enter_context(nc.sbuf_tensor(name, shape, dt))

        def sem(name):
            return ctx.enter_context(nc.semaphore(name))

        w1h = sb("w1h", [ONE + 1, NE * HID], F16)
        w1l = sb("w1l", [ONE + 1, NE * HID], F16)
        w2s = sb("w2s", [P, NE * HT, 2, D], F16)
        wg_raw = sb("wg_raw", [ONE + 1, NE])
        wgh = sb("wgh", [ONE + 1, NE], F16)
        wgl = sb("wgl", [ONE + 1, NE], F16)
        b2a = sb("b2a", [P, TT, D])
        b2c = sb("b2c", [P, TT, D])
        watt = sb("watt", [D, 3, D])
        batt = sb("batt", [ONE + 1, 3 * D])
        wqh = sb("wqh", [ONE + 1, 3 * D], F16)
        wql = sb("wql", [ONE + 1, 3 * D], F16)
        wpad = sb("wpad", [D, 2, TR, 32])
        wp = sb("wp", [D, 2, D])
        ident = sb("ident", [P, P])
        identb = sb("identb", [P, P], BF16)
        mask_q = sb("mask_q", [P, P], BF16)
        mask_k = sb("mask_k", [P, P], BF16)
        group = sb("group", [D, D])
        expert = sb("expert", [P, TT, 8], I32)
        power = sb("power", [P, TT])
        epsilon = sb("epsilon", [P, TT])

        xin = sb("xin", [P, TT, D])
        xt = sb("xt", [D, T])
        gst = sb("gst", [D, NC, 6])
        gmv = sb("gmv", [D, 2])
        gmean = sb("gmean", [D, 1])
        gdev = sb("gdev", [D, 1])
        gspread = sb("gspread", [D, 1])
        gvar = sb("gvar", [D, 1])
        grstd = sb("grstd", [D, 1])
        xah = sb("xah", [ONE + 1, T], F16)
        xal = sb("xal", [ONE + 1, T], F16)
        acc = sb("acc", [P, TT, D])
        x1 = sb("x1", [P, TT, D])
        hid = sb("hid", [P, HT, CH])
        hidh = sb("hidh", [P, 2, HT, CH], F16)
        hidl = sb("hidl", [P, 2, HT, CH], F16)

        class Routing:
            def __init__(self, n):
                self.score = sb(f"score{n}", [P, TT, 8])
                self.top = sb(f"top{n}", [P, TT, 8])
                self.idx = sb(f"idx{n}", [P, TT, 8], U32)
                self.shifted = sb(f"shifted{n}", [P, TT, 8])
                self.ex = sb(f"ex{n}", [P, TT, 8])
                self.prob = sb(f"prob{n}", [P, TT, 8])
                self.first = sb(f"first{n}", [P, TT, 8])
                self.second = sb(f"second{n}", [P, TT, 8])
                self.total = sb(f"total{n}", [P, TT])
                self.inv = sb(f"inv{n}", [P, TT])
                self.gates = sb(f"gates{n}", [P, 2 * TT, 8])
                self.gt = sb(f"gt{n}", [P, P])

        ra, rc_ = Routing("a"), Routing("c")

        st = sb("st", [P, TT, 6])
        mv1 = sb("mv1", [P, TT, 2])
        mv2 = sb("mv2", [P, TT, 2])
        rstd1 = sb("rstd1", [P, TT])
        rstd2 = sb("rstd2", [P, TT])
        xn1 = sb("xn1", [P, TT, D])
        xn2 = sb("xn2", [P, TT, D])
        xbh = sb("xbh", [ONE + 1, T], F16)
        xbl = sb("xbl", [ONE + 1, T], F16)
        qk_h = sb("qk_h", [D, 2, T], F16)
        qk_l = sb("qk_l", [D, 2, T], F16)
        mpart = sb("mpart", [P, H, TT, 2])
        mneg = sb("mneg", [P, P])
        mth = sb("mth", [H * TT, P], F16)
        mtl = sb("mtl", [H * TT, P], F16)
        yt = sb("yt", [D, 2, T])
        sums = sb("sums", [H * TT, P])
        rsum = sb("rsum", [H * TT, P])
        rb = sb("rb", [D, 2, T])
        x1r = sb("x1r", [P, TT, D])

        x2 = sb("x2", [P, TT, D])
        xch = sb("xch", [ONE + 1, T], F16)
        xcl = sb("xcl", [ONE + 1, T], F16)
        xo = sb("xo", [P, TT, D])

        with nc.sbuf_tensor("w1_raw", [ONE + 1, NE * HID], F32) as w1_raw, \
                nc.sbuf_tensor("w2_raw", [P, NE * HT, D], F32) as w2_raw:
            pass
        qs = sb("qs", [MROW + 2, H, T], F16)
        ks = sb("ks", [MROW + 2, H, T], F16)
        vaug = sb("vaug", [P, TT, H, 32])
        probs = sb("probs", [P, 3, TR, CH])

        qk_dram = nc.dram_tensor("qk_dram", (2, 2, D, T), F16, kind="Internal").ap()
        rsum_dram = nc.dram_tensor("rsum_dram", (H, T), F32, kind="Internal").ap()

        ps_u = [ctx.enter_context(nc.psum_tensor(f"ps_u{i}", [P, CH], F32)) for i in range(2)]
        ps_y = [ctx.enter_context(nc.psum_tensor(f"ps_y{i}", [P, CH], F32)) for i in range(2)]
        ps_r = [ctx.enter_context(nc.psum_tensor(f"ps_r{i}", [P, CH], F32)) for i in range(3)]
        ps_m = ctx.enter_context(nc.psum_tensor("ps_m", [P, CH], F32))

        def operand_c(b):
            last = isinstance(b.value(1, 0), int) and b.value(1, 0) == NIMG - 1
            return (xah, xal) if last else (xch, xcl)

        soft_banks = ps_r + ps_u

        def soft_bank(k):
            return soft_banks[k % len(soft_banks)]

        wg_loaded, b2a_loaded, b2c_loaded = sem("wg_loaded"), sem("b2a_loaded"), sem("b2c_loaded")
        watt_loaded, wproj_loaded = sem("watt_loaded"), sem("wproj_loaded")
        w1_loaded = [sem(f"w1_loaded{i}") for i in range(W1_PARTS)]
        w2_loaded = [sem(f"w2_loaded{i}") for i in range(W1_PARTS)]
        zeroed = sem("zeroed")
        zeroed_late = sem("zeroed_late")
        consts = sem("consts")
        ident_ready = sem("ident_ready")
        wg_ready = sem("wg_ready")
        w1_ready = sem("w1_ready")
        w2_ready = sem("w2_ready")
        watt_ready = sem("watt_ready")
        m_full, m_free = sem("m_full"), sem("m_free")
        up_full, h_ready = sem("up_full"), sem("h_ready")
        hl_ready = sem("hl_ready")
        y_full, y_free = sem("y_full"), sem("y_free")
        mx_full, mx_free = sem("mx_full"), sem("mx_free")
        s_full, p_ready = sem("s_full"), sem("p_ready")
        pv_step = sem("pv_step")
        pv_free = sem("pv_free")
        x_loaded = sem("x_loaded")
        xt_free = sem("xt_free")
        gn_var, gn_rstd = sem("gn_var"), sem("gn_rstd")
        ln1_var, ln1_rstd = sem("ln1_var"), sem("ln1_rstd")
        ln2_var, ln2_rstd = sem("ln2_var"), sem("ln2_rstd")
        gn_in = sem("gn_in")
        xn1_ready, xn2_ready = sem("xn1_ready"), sem("xn2_ready")
        xb_ready, xc_ready = sem("xb_ready"), sem("xc_ready")
        sub_a, exp_a, gates_a, gt_a = sem("sub_a"), sem("exp_a"), sem("gates_a"), sem("gt_a")
        sub_c, exp_c, gates_c, gt_c = sem("sub_c"), sem("exp_c"), sem("gates_c"), sem("gt_c")
        acc_ready = sem("acc_ready")
        qk_split, qk_out, qk_stacked = sem("qk_split"), sem("qk_out"), sem("qk_stacked")
        v_ready = sem("v_ready")
        hi_ready = sem("hi_ready")
        mneg_ready, m_split, m_stacked = sem("mneg_ready"), sem("m_split"), sem("m_stacked")
        yt_ready, sums_in, rsum_ready = sem("yt_ready"), sem("sums_in"), sem("rsum_ready")
        rsum_out, rb_in, yn_ready = sem("rsum_out"), sem("rb_in"), sem("yn_ready")
        x2_ready, x1r_ready = sem("x2_ready"), sem("x1r_ready")
        xo_ready, out_done = sem("xo_ready"), sem("out_done")

        QK_DMAS = 2 * 3

        x_d = x.rearrange("b (t q) w c -> b (q w) t c", t=TT)
        out_d = out.rearrange("b (t q) w c -> b (q w) t c", t=TT)

        block = ctx.enter_context(nc.Block())

        @block.sync
        def _(sp):
            sp.dma_start(wg_raw[0:D, 0:EA], cWg).then_inc(wg_loaded, 16)
            sp.dma_start(wg_raw[D:D + 1, 0:EA], cbg.rearrange("(a e) -> a e", a=1)).then_inc(wg_loaded, 16)
            sp.dma_start(wg_raw[0:D, EA:NE], fWg).then_inc(wg_loaded, 16)
            sp.dma_start(wg_raw[D:D + 1, EA:NE], fbg.rearrange("(a e) -> a e", a=1)).then_inc(wg_loaded, 16)
            raw = w1_raw[:].rearrange("d (e f) -> d e f", e=NE)

            def load_w1(part):
                e = 2 * part
                w, b, e0 = (cW1, cb1, e) if e < EA else (fW1, fb1, e - EA)
                sp.dma_start(raw[0:D, e:e + 2, :], w[e0:e0 + 2].rearrange("e d f -> d e f")
                             ).then_inc(w1_loaded[part], 16)
                sp.dma_start(raw[D:D + 1, e:e + 2, :], b[e0:e0 + 2].rearrange("(a e) f -> a e f", a=1)
                             ).then_inc(w1_loaded[part], 16)

            def load_w2(part):
                e = 2 * part
                w, e0 = (cW2, e) if e < EA else (fW2, e - EA)
                sp.dma_start(w2_raw[:, e * HT:(e + 2) * HT, :], w[e0:e0 + 2].rearrange("e (j p) o -> p (e j) o", p=P)
                             ).then_inc(w2_loaded[part], 16)

            for part in range(2):
                load_w1(part)
                load_w2(part)
            sp.wait_ge(zeroed, 1)
            for t in range(TT):
                sp.dma_start(b2a[8 * t:8 * t + EA, t, :], cb2).then_inc(b2a_loaded, 16)
            for part in range(2, W1_PARTS):
                load_w1(part)
                load_w2(part)
            sp.dma_start(watt[:], w_attn.rearrange("(s o) i -> o s i", s=3)).then_inc(watt_loaded, 16)
            sp.dma_start(batt[D:D + 1, :], b_attn.rearrange("(a o) -> a o", a=1)).then_inc(watt_loaded, 16)
            for t in range(2):
                sp.dma_start(wpad[:, t, :, 0:HD],
                             w_proj[:, t * TR * HD:(t + 1) * TR * HD].rearrange("o (g d) -> o g d", g=TR)
                             ).then_inc(wproj_loaded, 16)
            sp.dma_start(wpad[:, 0, 0, HD:HD + 1], b_proj.rearrange("(o a) -> o a", a=1)).then_inc(wproj_loaded, 16)
            for t in range(TT):
                sp.dma_start(b2c[8 * t:8 * t + EC, t, :], fb2).then_inc(b2c_loaded, 16)
            sp.wait_ge(zeroed_late, 1)

            def stack_qk(s, b):
                wait(sp, qk_split, b.value(2, s + 1))
                for n, part in enumerate((qk_h, qk_l)):
                    sp.dma_start(qk_dram[n, s], part[:, s, :]).then_inc(qk_out, 16)
                if s == 0:
                    wait(sp, s_full, b.value(SU, 0))
                wait(sp, qk_out, b.value(64, 32 * (s + 1)))
                dst, parts = ((qs, (0, 1, 0)), (ks, (0, 0, 1)))[s]
                for n, part in enumerate(parts):
                    sp.dma_start(dst[HD * n:HD * (n + 1), :, :],
                                 qk_dram[part, s].rearrange("(h d) t -> d h t", h=H)).then_inc(qk_stacked, 16)

            def stack_maxima(b):
                wait(sp, m_split, b.value(1, 1))
                for n, part in enumerate((mth, mtl)):
                    sp.dma_start(qs[MROW + n:MROW + n + 1, :, :].rearrange("a h (i q) -> a (h i) q", q=P),
                                 part[:]).then_inc(m_stacked, 16)

            def spread_sums(b):
                wait(sp, yt_ready, b.value(1, 1))
                for t in range(2):
                    for g in range(TR):
                        n = (t * TR + g) * TT
                        sp.dma_start(sums[n:n + TT, :], yt[32 * g + HD:32 * g + HD + 1, t, :]
                                     .rearrange("a (i q) -> a i q", q=P)).then_inc(sums_in, 16)
                wait(sp, rsum_ready, b.value(1, 1))
                sp.dma_start(rsum_dram.rearrange("h (i q) -> (h i) q", q=P), rsum[:]).then_inc(rsum_out, 16)
                wait(sp, rsum_out, b.value(16, 16))
                for g in range(TR):
                    sp.dma_start(rb[32 * g:32 * g + 32, :, :], rsum_dram.rearrange("(t g) q -> g t q", g=TR)[g:g + 1]
                                 .partition_broadcast(32)).then_inc(rb_in, 16)

            def chore(name, k, b):
                if name == "qk" and k % NC == NC - 1:
                    stack_qk(k // NC, b)
                if name == "maxima":
                    stack_maxima(b)

            def iteration(it, moe_a, attend, moe_c):
                for _, _, phase, slots in rounds(moe_a, moe_c):
                    for slot in slots:
                        for name, k, b in chores(it, phase, slot):
                            chore(name, k, b)
                for n in range(STEPS + 1):
                    for name, k, b in chores(it, 2, n):
                        chore(name, k, b)
                if attend:
                    spread_sums(Image(it, -1))

            walk(sp, [], iteration)

        @block.gpsimd
        def _(pool):
            g = nc.gpsimd
            g.memset(ident[:], 0.0)
            pool.drain()
            g.affine_select(out=ident[:], in_=ident[:], compare_op=ALU.not_equal, fill=1.0, base=0,
                            pattern=[[-1, P]], channel_multiplier=1)
            pool.drain().then_inc(ident_ready, 1)
            g.memset(group[:], 1.0 / 3.0)
            g.iota(expert[:], pattern=[[0, TT], [1, 8]], base=0, channel_multiplier=0)
            for tile, value in ((epsilon, 1e-5), (power, -0.5), (ra.gates, 0.0), (rc_.gates, 0.0),
                                (rc_.prob, -1.0), (b2a, 0.0), (b2c, 0.0), (wpad, 0.0)):
                g.memset(tile[:], value)
            pool.drain()
            for tile, value in ((identb, 0.0), (mask_q, 0.0), (mask_k, 0.0), (mpart, NEG), (mneg, 0.0)):
                g.memset(tile[:], value)
            pool.drain()
            for tile, value in ((xah, 1.0), (xal, 0.0), (xbh, 1.0), (xbl, 0.0), (xch, 1.0), (xcl, 0.0)):
                g.memset(tile[ONE:ONE + 1, :], value)
            pool.drain()
            grouped = group[:].rearrange("p (a r) -> p a r", r=3)
            g.affine_select(out=grouped, in_=grouped, compare_op=ALU.is_ge, fill=0.0, base=0,
                            pattern=[[-3, D // 3], [0, 3]], channel_multiplier=1)
            pool.drain()
            g.affine_select(out=grouped, in_=grouped, compare_op=ALU.is_ge, fill=0.0, base=2,
                            pattern=[[3, D // 3], [0, 3]], channel_multiplier=-1)
            pool.drain().then_inc(zeroed, 1)
            g.affine_select(out=identb[:], in_=identb[:], compare_op=ALU.not_equal, fill=1.0, base=0,
                            pattern=[[-1, P]], channel_multiplier=1)
            g.affine_select(out=mask_q[:], in_=mask_q[:], compare_op=ALU.is_ge, fill=NEG, base=0,
                            pattern=[[-1, P]], channel_multiplier=1)
            g.affine_select(out=mask_k[:], in_=mask_k[:], compare_op=ALU.is_ge, fill=NEG, base=0,
                            pattern=[[1, P]], channel_multiplier=-1)
            pool.drain().then_inc(consts, 1)

            def rstd(dst, var, ready, done, b):
                pool.wait_ge(ready, b.value(1, 1))
                n = var.shape[0]
                g.tensor_tensor(dst, var, epsilon[0:n, 0:dst.shape[1]], ALU.add)
                pool.drain()
                g.tensor_tensor(dst, dst, power[0:n, 0:dst.shape[1]], ALU.pow).then_inc(done, 1)

            def chore(name, k, b):
                if name == "gn_spread":
                    rstd(grstd[:], gvar[:], gn_var, gn_rstd, b)
                if name == "ln1" and k == 1:
                    rstd(rstd1[:], mv1[:, :, 1], ln1_var, ln1_rstd, b)
                if name == "ln2" and k == 1:
                    rstd(rstd2[:], mv2[:, :, 1], ln2_var, ln2_rstd, b)

            grp = Count(GA + GC)

            def iteration(it, moe_a, attend, moe_c):
                for up, _, phase, slots in rounds(moe_a, moe_c):
                    for slot in slots:
                        j = slot % TC
                        if up and j < HT:
                            pool.wait_ge(h_ready, grp.value(HT, j + 1))
                            g.tensor_tensor(hidl[:, grp.k % 2, j, :], hid[:, j, :], hidh[:, grp.k % 2, j, :],
                                            ALU.subtract).then_inc(hl_ready, 1)
                        for name, k, b in chores(it, phase, slot):
                            chore(name, k, b)
                    if up:
                        grp.k += 1
                for n in range(STEPS + 1):
                    for name, k, b in chores(it, 2, n):
                        chore(name, k, b)

            for name in PROLOGUE:
                chore(name, 0, Image(0, 0))
            walk(pool, [grp], iteration)

        @block.tensor
        def _(pe):
            m, grp = Count(shared_uses()), Count(GA + GC)

            def mm(dst, lhsT, rhs, start=True, stop=True):
                return nc.tensor.matmul(dst, lhsT, rhs, start=start, stop=stop, skip_group_check=True)

            def split(dst, wh, wl, xh, xl, moving_x):
                pairs = ((wh, xh), (wl, xh), (wh, xl))
                for n, (w, v) in enumerate(pairs):
                    a, b = (w, v) if moving_x else (v, w)
                    last = mm(dst, a, b, n == 0, n == 2)
                return last

            def shared():
                wait(pe, m_free, m.value())
                m.k += 1

            def turn(src, c):
                shared()
                for i in range(TC):
                    last = nc.tensor.transpose(ps_m[0:D, P * i:P * (i + 1)], src[:, TC * c + i, :], ident[:])
                last.then_inc(m_full, 1)

            def logits(xh, xl, e0, n):
                shared()
                for t in range(TT):
                    tok = slice(P * t, P * (t + 1))
                    last = split(ps_m[:, 8 * t:8 * t + n], wgh[:, e0:e0 + n], wgl[:, e0:e0 + n],
                                 xh[:, tok], xl[:, tok], False)
                last.then_inc(m_full, 1)

            def gates_turn(r, ready, b):
                pe.wait_ge(ready, b.value(1, 1))
                shared()
                nc.tensor.transpose(ps_m[:, 0:P], r.gates[:].rearrange("p t e -> p (t e)"), ident[:]
                                    ).then_inc(m_full, 1)

            def bias2(r, b2, ready, b, c):
                pe.wait_ge(ready, b.value(1, 1))
                shared()
                mm(ps_m[:, 0:TC * D], r.gt[:],
                   b2[:, TC * c:TC * (c + 1), :].rearrange("p t d -> p (t d)")).then_inc(m_full, 1)

            def group_mean(part, b):
                pe.wait_ge(gn_in, b.value(2, part))
                shared()
                mm(ps_m[0:D, 0:1], group[:], gmv[:, 0:1] if part == 1 else gspread[:]).then_inc(m_full, 1)

            def first_layer(it, group, j):
                xh, xl = (xah, xal) if group.moe == 0 else operand_c(image_c(it))
                e, c = EA * group.moe + group.e, group.c
                wait(pe, h_ready, grp.value(HT, j - 1))
                w = slice((e * HT + j) * P, (e * HT + j + 1) * P)
                tok = slice(CH * c, CH * (c + 1))
                bank = ps_u[(HT * grp.k + j) % 2]
                split(bank[:], w1h[:, w], w1l[:, w], xh[:, tok], xl[:, tok], True).then_inc(up_full, 1)

            def second_layer(group, i):
                e = EA * group.moe + group.e
                n = grp.k - 1
                out = ps_y[n % 2][:, D * i:D * (i + 1)]
                tok = slice(P * i, P * (i + 1))
                if i == 0:
                    pe.wait_ge(h_ready, grp.value(HT, 0))
                    wait(pe, y_free, grp.value(1, -2))
                for j in range(HT):
                    for part in range(2):
                        mm(out, hidh[:, n % 2, j, tok], w2s[:, e * HT + j, part, :], j == 0 and part == 0, False)
                if i == 0:
                    pe.wait_ge(hl_ready, grp.value(HT, 0))
                for j in range(HT):
                    last = mm(out, hidl[:, n % 2, j, tok], w2s[:, e * HT + j, 0, :], False, j == HT - 1)
                if i == TC - 1:
                    last.then_inc(y_full, 1)

            def moes(it, moe_a, moe_c):
                starts = isinstance(it, int) and it == 0
                first = True
                if moe_a:
                    pe.wait_ge(xt_free, Image(it, 0).value(1, 1))
                for up, down, phase, slots in rounds(moe_a, moe_c):
                    if starts and up and up.c == 0 and up.e % 2 == 0:
                        pe.wait_ge(w1_ready, up.e // 2 + 1)
                    if starts and down and down.c == 0 and down.e % 2 == 0:
                        pe.wait_ge(w2_ready, down.e // 2 + 1)
                    if starts and phase == 1:
                        pe.wait_ge(w1_ready, W1_PARTS)
                        pe.wait_ge(w2_ready, W1_PARTS)
                        pe.wait_ge(b2c_loaded, 16 * TT)
                        pe.wait_ge(consts, 1)
                        pe.wait_ge(watt_ready, 1)
                        pe.wait_ge(zeroed_late, 1)
                    for slot in slots:
                        j = slot % TC
                        if up and j < HT:
                            first_layer(it, up, j)
                        if down and first:
                            if not (isinstance(it, int) and it > NIMG + 1):
                                wait(pe, pv_free, Image(it, -2).value(4, 4))
                            first = False
                        if down:
                            for i in ((), (0,), (1,), (2, 3))[j]:
                                second_layer(down, i)
                        run_chores(m, chore, chores(it, phase, slot))
                    if up:
                        grp.k += 1

            def qk(s, c, b):
                pe.wait_ge(xb_ready, b.value(NC, NC))
                w = slice(D * s, D * (s + 1))
                shared()
                tok = slice(CH * c, CH * (c + 1))
                split(ps_m[0:D, :], wqh[:, w], wql[:, w], xbh[:, tok], xbl[:, tok], True).then_inc(m_full, 1)

            def values(c):
                w = slice(2 * D, 3 * D)
                shared()
                for i in range(TC):
                    tok = slice(P * (TC * c + i), P * (TC * c + i + 1))
                    last = split(ps_m[:, D * i:D * (i + 1)], wqh[:, w], wql[:, w], xbh[:, tok], xbl[:, tok], False)
                last.then_inc(m_full, 1)

            def maximum(b, k):
                h, i, part = MAX_UNITS[k]
                if k == 0:
                    pe.wait_ge(qk_stacked, b.value(16 * QK_DMAS, 16 * QK_DMAS))
                    wait(pe, p_ready, b.value(SU, 0))
                wait(pe, mx_free, b.value(MAXU, k - 2))
                k0 = CH * part
                w = min(CH, P * (i + 1) - k0)
                diagonal = k0 + w == P * (i + 1)
                bank = ps_r[k % 3]
                last = mm(bank[:, 0:w], qs[0:MROW, h, P * i:P * (i + 1)], ks[0:MROW, h, k0:k0 + w],
                          True, not diagonal)
                if diagonal:
                    last = mm(bank[:, w - P:w], identb[:], mask_q[:], False, True)
                last.then_inc(mx_full, 1)

            def maxima_turn(b):
                pe.wait_ge(mneg_ready, b.value(1, 1))
                shared()
                nc.tensor.transpose(ps_m[:, 0:P], mneg[:], ident[:]).then_inc(m_full, 1)

            def soft_scores(b, n):
                t, c, j = SOFT_STEPS[n]
                q0 = max(CH * c, P * j)
                w = CH * (c + 1) - q0
                for g in range(TR):
                    k = n * TR + g
                    if n == 0 and g == 0:
                        pe.wait_ge(m_stacked, b.value(32, 32))
                        pe.wait_ge(mx_free, b.value(MAXU, MAXU))
                    if k == len(ps_r):
                        pe.wait_ge(h_ready, grp.value(HT, 0))
                    if k >= len(soft_banks):
                        pe.wait_ge(p_ready, b.value(SU, k - len(soft_banks) + 1))
                    h = t * TR + g
                    diagonal = P * j >= CH * c
                    last = mm(soft_bank(k)[:, 0:w], ks[0:MROW + 2, h, P * j:P * (j + 1)],
                              qs[0:MROW + 2, h, q0:q0 + w], True, not diagonal)
                    if diagonal:
                        last = mm(soft_bank(k)[:, 0:P], identb[:], mask_k[:], False, True)
                    last.then_inc(s_full, 1)

            def soft_values(b, n):
                t, c, j = SOFT_STEPS[n]
                q0 = max(CH * c, P * j)
                w = CH * (c + 1) - q0
                off = q0 - CH * c
                pe.wait_ge(p_ready, b.value(SU, (n + 1) * TR))
                if n == 0:
                    pe.wait_ge(v_ready, b.value(NC, NC))
                if j == 0:
                    wait(pe, pv_free, b.value(4, 2 * t + c - 1))
                for g in range(TR):
                    last = mm(ps_y[(2 * t + c) % 2][32 * g:32 * g + 32, off:off + w],
                              vaug[:, j, t * TR + g, :], probs[:, n % 3, g, 0:w],
                              j == 0, j == TC * (c + 1) - 1)
                last.then_inc(pv_step, 1)

            def softmax(it, b, attend):
                for n in range(STEPS + 2):
                    if n < STEPS and attend:
                        soft_scores(b, n)
                    if n == 2 and attend:
                        wait(pe, y_free, grp.value())
                    if n > 1 and attend:
                        soft_values(b, n - 2)
                    run_chores(m, chore, chores(it, 2, n))

            def project(c):
                shared()
                for i in range(TC):
                    q = P * (TC * c + i)
                    for t in range(2):
                        last = mm(ps_m[:, D * i:D * (i + 1)], yt[:, t, q:q + P], wp[:, t, :], t == 0, t == 1)
                last.then_inc(m_full, 1)

            def chore(name, k, b):
                if name == "x_turn":
                    if k == 0:
                        pe.wait_ge(x_loaded, b.value(16, 16))
                    turn(xin, k)
                if name in ("gn_mean", "gn_spread"):
                    if name == "gn_mean" and isinstance(b.value(1, 0), int) and b.value(1, 0) == 0:
                        pe.wait_ge(zeroed, 1)
                    group_mean(1 if name == "gn_mean" else 2, b)
                if name == "logits_a":
                    if isinstance(b.value(1, 0), int) and b.value(1, 0) == 0:
                        pe.wait_ge(wg_ready, 1)
                    pe.wait_ge(xt_free, b.value(1, 1))
                    logits(xah, xal, 0, EA)
                if name == "gates_a":
                    gates_turn(ra, gates_a, b)
                if name == "bias_a":
                    bias2(ra, b2a, gt_a, b, k)
                if name == "x1_turn":
                    pe.wait_ge(xn1_ready, b.value(NC, k + 1))
                    turn(xn1, k)
                if name == "qk":
                    qk(k // NC, k % NC, b)
                if name == "val":
                    values(k)
                if name == "max":
                    maximum(b, k)
                if name == "maxima":
                    maxima_turn(b)
                if name == "project":
                    pe.wait_ge(yn_ready, b.value(2, 2))
                    project(k)
                if name == "x2_turn":
                    pe.wait_ge(xn2_ready, b.value(NC, k + 1))
                    turn(xn2, k)
                if name == "logits_c":
                    pe.wait_ge(xc_ready, b.value(NC, NC))
                    logits(*operand_c(b), EA, EC)
                if name == "gates_c":
                    gates_turn(rc_, gates_c, b)
                if name == "bias_c":
                    bias2(rc_, b2c, gt_c, b, k)
                if name == "turn_watt":
                    if k == 0:
                        pe.wait_ge(watt_loaded, 32)
                    shared()
                    nc.tensor.transpose(ps_m[0:D, 0:D], watt[:, k, :], ident[0:D, 0:D]).then_inc(m_full, 1)
                if name == "turn_wp":
                    if k == 0:
                        pe.wait_ge(wproj_loaded, 48)
                    shared()
                    nc.tensor.transpose(ps_m[0:D, 0:D], wpad[:, k, :, :].rearrange("o g d -> o (g d)"),
                                        ident[0:D, 0:D]).then_inc(m_full, 1)

            def iteration(it, moe_a, attend, moe_c):
                if not (isinstance(it, int) and it > NIMG + 1):
                    wait(pe, p_ready, Image(it, -2).value(SU, SU))
                moes(it, moe_a, moe_c)
                softmax(it, Image(it, -1), attend)

            pe.wait_ge(ident_ready, 1)
            prologue(m, chore)
            pe.wait_ge(b2a_loaded, 16 * TT)
            walk(pe, [m, grp], iteration)

        @block.scalar
        def _(act):
            m, grp = Count(shared_uses()), Count(GA + GC)
            a = nc.scalar

            def moes(it, moe_a, moe_c):
                for up, _, phase, slots in rounds(moe_a, moe_c):
                    for slot in slots:
                        j = slot % TC
                        if up and j < HT:
                            act.wait_ge(up_full, grp.value(HT, j + 1))
                            if j == 0:
                                wait(act, y_full, grp.value(1, -1))
                            wait(act, hl_ready, grp.value(HT, j + 1 - HT))
                            bank = ps_u[(HT * grp.k + j) % 2]
                            a.activation(hid[:, j, :], bank[:], ACT.Gelu, scale=1.0 / WS)
                            a.activation(hidh[:, grp.k % 2, j, :], bank[:], ACT.Gelu, scale=1.0 / WS
                                         ).then_inc(h_ready, 1)
                        run_chores(m, chore, chores(it, phase, slot))
                    if up:
                        grp.k += 1

            def exponentials(r, ready, done, n, b):
                act.wait_ge(ready, b.value(1, 1))
                a.activation(r.ex[:, :, 0:n], r.shifted[:, :, 0:n], ACT.Exp, scale=1.0 / WS).then_inc(done, 1)

            def x_load(b):
                wait(act, acc_ready, b.value(1, 0))
                act.dma_start(xin[:], x_d[b.value(1, 0)]).then_inc(x_loaded, 16)

            def store(b):
                act.wait_ge(xo_ready, b.value(1, 1))
                act.dma_start(out_d[b.value(1, 0)], xo[:]).then_inc(out_done, 16)

            def softmax(it, b, attend):
                for n in range(STEPS + 1):
                    if attend and n < STEPS:
                        t, c, j = SOFT_STEPS[n]
                        w = CH * (c + 1) - max(CH * c, P * j)
                        if n < 3:
                            wait(act, pv_step, b.value(STEPS, 0))
                        else:
                            act.wait_ge(pv_step, b.value(STEPS, n - 2))
                        for g in range(TR):
                            k = n * TR + g
                            act.wait_ge(s_full, b.value(SU, k + 1))
                            a.activation(probs[:, n % 3, g, 0:w], soft_bank(k)[:, 0:w], ACT.Exp,
                                         scale=float(HD) ** -0.5).then_inc(p_ready, 1)
                    run_chores(m, chore, chores(it, 2, n))

            def chore(name, k, b):
                if name == "x_load":
                    x_load(b)
                if name == "x_turn":
                    if k == 0:
                        wait(act, xt_free, b.value(1, 0))
                    m.k += 1
                    act.wait_ge(m_full, m.value())
                    a.activation(xt[:, CH * k:CH * (k + 1)], ps_m[0:D, :], ACT.Copy).then_inc(m_free, 1)
                if name in ("x1_turn", "x2_turn", "qk"):
                    c = k % NC
                    high, unscale = {"x1_turn": (xbh[0:D, :], 1.0), "x2_turn": (operand_c(b)[0][0:D, :], 1.0),
                                     "qk": (qk_h[:, k // NC, :], 1.0 / WS)}[name]
                    if name == "x1_turn" and k == 0:
                        wait(act, v_ready, b.value(NC, 0))
                    if name == "qk" and k == 0:
                        wait(act, qk_out, b.value(64, 0))
                    m.k += 1
                    act.wait_ge(m_full, m.value())
                    a.activation(high[:, CH * c:CH * (c + 1)], ps_m[0:D, :], ACT.Copy, scale=unscale
                                 ).then_inc(hi_ready, 1)
                if name == "exp_a":
                    exponentials(ra, sub_a, exp_a, EA, b)
                if name == "exp_c":
                    exponentials(rc_, sub_c, exp_c, EC, b)
                if name == "val":
                    if k == 0:
                        wait(act, pv_step, b.value(STEPS, 0))
                        if isinstance(b.value(1, 0), int) and b.value(1, 0) == 0:
                            act.wait_ge(zeroed_late, 1)
                    m.k += 1
                    act.wait_ge(m_full, m.value())
                    a.activation(vaug[:, TC * k:TC * (k + 1), :, 0:HD],
                                 ps_m[:, 0:TC * D].rearrange("p (t h d) -> p t h d", t=TC, h=H),
                                 ACT.Copy, scale=1.0 / WS)
                    act.drain().then_inc(m_free, 1)
                    act.nop().then_inc(v_ready, 1)
                if name == "keep_x1":
                    wait(act, x2_ready, b.value(1, 0))
                    act.wait_ge(ln1_var, b.value(1, 1))
                    a.activation(x1r[:], x1[:], ACT.Copy).then_inc(x1r_ready, 1)
                if name == "store":
                    store(b)

            def iteration(it, moe_a, attend, moe_c):
                moes(it, moe_a, moe_c)
                softmax(it, Image(it, -1), attend)

            x_load(Image(0, 0))
            prologue(m, chore)
            walk(act, [m, grp], iteration)
            act.wait_ge(out_done, 16 * NIMG)

        @block.vector
        def _(dve):
            m, grp = Count(shared_uses()), Count(GA + GC)
            his = Count(sum(name in ("x1_turn", "x2_turn", "qk") for phase in schedule(None)
                            for at in phase.values() for name, _, _ in at))
            v = nc.vector

            def split(hi, lo, src, scale):
                v.tensor_scalar(hi, src, scale, None, ALU.mult)
                dve.drain()
                return v.scalar_tensor_tensor(out=lo, in0=src, scalar=scale, in1=hi, op0=ALU.mult,
                                              op1=ALU.subtract)

            def shared():
                m.k += 1
                dve.wait_ge(m_full, m.value())

            def low_part(lo, hi, scale):
                shared()
                his.k += 1
                dve.wait_ge(hi_ready, his.value())
                return v.scalar_tensor_tensor(out=lo, in0=ps_m[0:D, :], scalar=scale, in1=hi, op0=ALU.mult,
                                              op1=ALU.subtract).then_inc(m_free, 1)

            def split_turned(xh, xl, c, ready):
                tok = slice(CH * c, CH * (c + 1))
                low_part(xl[0:D, tok], xh[0:D, tok], 1.0)
                dve.drain().then_inc(ready, 1)

            def largest(r, values):
                for t in range(TT):
                    v.max(r.top[:, t, :], values[:, t, :])
                dve.drain()

            def largest_at(r, values):
                for t in range(TT):
                    v.max_index(r.idx[:, t, :], r.top[:, t, :], values[:, t, :])
                dve.drain()

            def top_two(r):
                for dst, n in ((r.first, 0), (r.second, 1)):
                    v.tensor_tensor(dst[:], expert[:], r.idx[:, :, n:n + 1].to_broadcast([P, TT, 8]), ALU.is_equal)
                dve.drain()
                v.tensor_tensor(r.first[:], r.first[:], r.second[:], ALU.add)

            def scores(r, n, ready):
                shared()
                v.tensor_copy(r.score[:, :, 0:n],
                              ps_m[:, 0:TT * 8].rearrange("p (t e) -> p t e", e=8)[:, :, 0:n]).then_inc(m_free, 1)
                dve.drain()
                v.tensor_reduce(r.total[:], r.score[:, :, 0:n], AX, ALU.max)
                dve.drain()
                v.tensor_tensor(r.shifted[:, :, 0:n], r.score[:, :, 0:n],
                                r.total[:].unsqueeze(2).to_broadcast([P, TT, n]), ALU.subtract).then_inc(ready, 1)

            def normalise(r, dst, src, n, eps, scale):
                v.tensor_reduce(r.total[:], src, AX, ALU.add)
                dve.drain()
                v.tensor_scalar(r.total[:], r.total[:], eps, scale, ALU.add, ALU.mult)
                dve.drain()
                v.reciprocal(r.inv[:], r.total[:])
                dve.drain()
                return v.tensor_tensor(dst, src, r.inv[:].unsqueeze(2).to_broadcast([P, TT, n]), ALU.mult)

            def gates_out(r, done, b):
                shared()
                v.tensor_scalar(r.gt[:], ps_m[:, 0:P], WS, None, ALU.mult).then_inc(m_free, 1)
                dve.drain().then_inc(done, 1)

            def combine(group, out):
                r, c, e = (ra, rc_)[group.moe], group.c, group.e
                dve.wait_ge(y_full, grp.value(1, 1))
                wait(dve, y_free, grp.value())
                for i in range(TC):
                    t = TC * c + i
                    last = v.scalar_tensor_tensor(out=out[:, t, :], in0=ps_y[grp.k % 2][:, D * i:D * (i + 1)],
                                                  scalar=r.gates[:, t, e:e + 1], in1=acc[:, t, :],
                                                  op0=ALU.mult, op1=ALU.add)
                last.then_inc(y_free, 1)
                grp.k += 1

            def moes(it, moe_a, moe_c):
                for up, down, phase, slots in rounds(moe_a, moe_c):
                    for slot in slots:
                        run_chores(m, chore, chores(it, phase, slot))
                    if down:
                        last = down.e == (EA, EC)[down.moe] - 1
                        if last and down.c == 0 and down.moe == 0:
                            wait(dve, x1r_ready, Image(it, 0).value(1, 0))
                        if last and down.c == 0 and down.moe == 1:
                            wait(dve, out_done, image_c(it).value(16, 0))
                        combine(down, (x1, xo)[down.moe] if last else acc)
                if moe_c:
                    dve.drain().then_inc(xo_ready, 1)

            def ln_stats(src, mv, ready, half):
                tiles = range(TC * half, TC * (half + 1))
                for t in tiles:
                    v.bn_stats(st[:, t, :], src[:, t, :])
                dve.drain()
                for t in tiles:
                    v.bn_aggr(mv[:, t, :], st[:, t, :])
                if half == 1:
                    dve.drain().then_inc(ready, 1)

            def ln_apply(dst, src, mv, rstd, got, ready, b, half):
                if half == 0:
                    dve.wait_ge(got, b.value(1, 1))
                for t in range(TC * half, TC * (half + 1)):
                    v.tensor_scalar(dst[:, t, :], src[:, t, :], mv[:, t, 0:1], rstd[:, t:t + 1],
                                    ALU.subtract, ALU.mult)
                dve.drain().then_inc(ready, 1)

            def split_qk(s, c, b):
                if s == 0 and c == 0:
                    wait(dve, qk_out, b.value(64, 0))
                tok = slice(CH * c, CH * (c + 1))
                low_part(qk_l[:, s, tok], qk_h[:, s, tok], 1.0 / WS)
                if c == NC - 1:
                    dve.drain().then_inc(qk_split, 1)

            def maximum(b, k):
                h, i, part = MAX_UNITS[k]
                w = min(CH, P * (i + 1) - CH * part)
                if k == 0 and isinstance(b.value(1, 0), int) and b.value(1, 0) == 0:
                    dve.wait_ge(zeroed_late, 1)
                dve.wait_ge(mx_full, b.value(MAXU, k + 1))
                v.tensor_reduce(mpart[:, h, i, part:part + 1], ps_r[k % 3][:, 0:w], AX, ALU.max
                                ).then_inc(mx_free, 1)

            def maxima(b):
                dve.drain()
                used = mneg[:, 0:H * TT]
                v.tensor_reduce(used.rearrange("p (h i) -> p h i", h=H), mpart[:], AX, ALU.max)
                dve.drain()
                v.tensor_scalar(used, used, -1.0 / MS, None, ALU.mult).then_inc(mneg_ready, 1)
                wait(dve, m_stacked, b.value(32, 0))
                shared()
                split(mth[:], mtl[:], ps_m[0:H * TT, 0:P], 1.0).then_inc(m_free, 1)
                dve.drain().then_inc(m_split, 1)

            def softmax(it, b, attend):
                ends = {TC: 0, TC + 2 * TC: 1, TC + 3 * TC: 2, 2 * (TC + 2 * TC): 3}
                for n in range(STEPS + 2):
                    run_chores(m, chore, chores(it, 2, n))
                    if attend and n - 1 in ends:
                        t, c = ends[n - 1] // NC, ends[n - 1] % NC
                        dve.wait_ge(pv_step, b.value(STEPS, n - 1))
                        v.tensor_copy(yt[:, t, CH * c:CH * (c + 1)], ps_y[ends[n - 1] % 2][0:D, :]).then_inc(pv_free, 1)
                if attend:
                    dve.drain().then_inc(yt_ready, 1)

            def chore(name, k, b):
                tiles = slice(TC * k, TC * (k + 1))
                if name == "split_gate":
                    dve.wait_ge(wg_loaded, 64)
                    dve.wait_ge(zeroed, 1)
                    split(wgh[:], wgl[:], wg_raw[:], WS)
                    dve.drain().then_inc(wg_ready, 1)
                if name == "split_w1":
                    dve.wait_ge(w1_loaded[k], 32)
                    w = slice(2 * HID * k, 2 * HID * (k + 1))
                    split(w1h[:, w], w1l[:, w], w1_raw[:, w], WS)
                    dve.drain().then_inc(w1_ready, 1)
                if name == "split_w2":
                    dve.wait_ge(w2_loaded[k], 16)
                    w = slice(2 * HT * k, 2 * HT * (k + 1))
                    split(w2s[:, w, 0, :], w2s[:, w, 1, :], w2_raw[:, w, :], WS)
                    dve.drain().then_inc(w2_ready, 1)
                if name == "zero":
                    tile, n = (qs, H // 3) if k < 3 else (ks, H // 3) if k < 6 else (vaug, TT // 2)
                    at = slice(n * (k % 3), n * (k % 3 + 1)) if k < 6 else slice(n * (k - 6), n * (k - 5))
                    v.memset(tile[:, at], 0.0)
                    if k == ZEROS - 1:
                        dve.drain()
                        v.memset(vaug[:, :, :, HD:HD + 1], 1.0)
                        v.memset(ks[MROW:MROW + 2, :, :], MS)
                        dve.drain().then_inc(zeroed_late, 1)
                if name == "turn_watt":
                    shared()
                    w = slice(D * k, D * (k + 1))
                    split(wqh[0:D, w], wql[0:D, w], ps_m[0:D, 0:D], WS).then_inc(m_free, 1)
                    if k == 0:
                        dve.wait_ge(watt_loaded, 32)
                        split(wqh[ONE:ONE + 1, :], wql[ONE:ONE + 1, :], batt[ONE:ONE + 1, :], WS)
                if name == "turn_wp":
                    shared()
                    v.tensor_copy(wp[:, k, :], ps_m[0:D, 0:D]).then_inc(m_free, 1)
                    if k == 1:
                        dve.drain().then_inc(watt_ready, 1)
                if name == "gn_stats":
                    dve.wait_ge(m_free, m.value())
                    for c in range(NC):
                        v.bn_stats(gst[:, c, :], xt[:, CH * c:CH * (c + 1)])
                    dve.drain()
                    v.bn_aggr(gmv[:], gst[:]).then_inc(gn_in, 1)
                if name == "gn_mean":
                    shared()
                    v.tensor_copy(gmean[:], ps_m[0:D, 0:1]).then_inc(m_free, 1)
                    dve.drain()
                    v.tensor_tensor(gdev[:], gmv[:, 0:1], gmean[:], ALU.subtract)
                    dve.drain()
                    v.scalar_tensor_tensor(out=gspread[:], in0=gdev[:], scalar=gdev[:], in1=gmv[:, 1:2],
                                           op0=ALU.mult, op1=ALU.add).then_inc(gn_in, 1)
                if name == "gn_spread":
                    shared()
                    v.tensor_copy(gvar[:], ps_m[0:D, 0:1]).then_inc(m_free, 1)
                    dve.drain().then_inc(gn_var, 1)
                if name == "gn_apply":
                    dve.wait_ge(gn_rstd, b.value(1, 1))
                    v.tensor_scalar(xt[:], xt[:], gmean[:], grstd[:], ALU.subtract, ALU.mult)
                    dve.drain()
                    v.tensor_copy(xah[0:D, :], xt[:])
                    dve.drain()
                    v.tensor_tensor(xal[0:D, :], xt[:], xah[0:D, :], ALU.subtract).then_inc(xt_free, 1)
                if name == "logits_a":
                    scores(ra, EA, sub_a)
                if name == "route_a" and k == 0:
                    largest(ra, ra.score)
                if name == "route_a" and k == 1:
                    largest_at(ra, ra.score)
                if name == "route_a" and k == 2:
                    top_two(ra)
                    dve.drain()
                    dve.wait_ge(exp_a, b.value(1, 1))
                    v.tensor_tensor(ra.prob[:], ra.ex[:], ra.first[:], ALU.mult)
                    dve.drain()
                    normalise(ra, ra.gates[:, 0:TT, :], ra.prob[:], EA, 0.0, WS).then_inc(gates_a, 1)
                if name == "gates_a":
                    gates_out(ra, gt_a, b)
                if name == "bias_a":
                    shared()
                    v.tensor_tensor(acc[:, tiles, :], ps_m[:, 0:TC * D].rearrange("p (t d) -> p t d", t=TC),
                                    xin[:, tiles, :], ALU.add).then_inc(m_free, 1)
                    if k == NC - 1:
                        dve.drain().then_inc(acc_ready, 1)
                if name == "ln1":
                    dve.drain()
                    ln_stats(x1, mv1, ln1_var, k)
                if name == "ln1_apply":
                    ln_apply(xn1, x1, mv1, rstd1, ln1_rstd, xn1_ready, b, k)
                if name == "x1_turn":
                    if k == 0:
                        wait(dve, v_ready, b.value(NC, 0))
                    split_turned(xbh, xbl, k, xb_ready)
                if name == "qk":
                    split_qk(k // NC, k % NC, b)
                if name == "max":
                    maximum(b, k)
                if name == "maxima":
                    maxima(b)
                if name == "sum_inverse":
                    wait(dve, rsum_out, b.value(16, 0))
                    dve.wait_ge(sums_in, b.value(16 * H, 16 * H))
                    v.reciprocal(rsum[:], sums[:]).then_inc(rsum_ready, 1)
                if name == "normalise_y":
                    dve.wait_ge(rb_in, b.value(16 * TR, 16 * TR))
                    v.tensor_tensor(yt[:, k, :], yt[:, k, :], rb[:, k, :], ALU.mult).then_inc(yn_ready, 1)
                if name == "project":
                    if k == 0:
                        dve.wait_ge(x1r_ready, b.value(1, 1))
                    shared()
                    v.tensor_tensor(x2[:, tiles, :], ps_m[:, 0:TC * D].rearrange("p (t d) -> p t d", t=TC),
                                    x1r[:, tiles, :], ALU.add).then_inc(m_free, 1)
                    if k == NC - 1:
                        dve.drain().then_inc(x2_ready, 1)
                if name == "ln2":
                    ln_stats(x2, mv2, ln2_var, k)
                if name == "ln2_apply":
                    ln_apply(xn2, x2, mv2, rstd2, ln2_rstd, xn2_ready, b, k)
                if name == "x2_turn":
                    split_turned(*operand_c(b), k, xc_ready)
                if name == "logits_c":
                    scores(rc_, EC, sub_c)
                if name == "route_c" and k == 0:
                    dve.wait_ge(exp_c, b.value(1, 1))
                    normalise(rc_, rc_.prob[:, :, 0:EC], rc_.ex[:, :, 0:EC], EC, 0.0, 1.0)
                    dve.drain()
                if name == "route_c" and k == 1:
                    largest(rc_, rc_.prob)
                if name == "route_c" and k == 2:
                    largest_at(rc_, rc_.prob)
                if name == "route_c" and k == 3:
                    top_two(rc_)
                    dve.drain()
                    v.tensor_tensor(rc_.ex[:, :, 0:EC], rc_.prob[:, :, 0:EC], rc_.first[:, :, 0:EC], ALU.mult)
                    dve.drain()
                    normalise(rc_, rc_.gates[:, 0:TT, 0:EC], rc_.ex[:, :, 0:EC], EC, 1e-9, WS).then_inc(gates_c, 1)
                if name == "gates_c":
                    gates_out(rc_, gt_c, b)
                if name == "bias_c":
                    dve.drain()
                    shared()
                    v.tensor_tensor(acc[:, tiles, :], ps_m[:, 0:TC * D].rearrange("p (t d) -> p t d", t=TC),
                                    x2[:, tiles, :], ALU.add).then_inc(m_free, 1)
                    if k == NC - 1:
                        dve.drain()

            def iteration(it, moe_a, attend, moe_c):
                moes(it, moe_a, moe_c)
                softmax(it, Image(it, -1), attend)

            prologue(m, chore)
            walk(dve, [m, grp, his], iteration)


_INS = ['x', 'L0_conv_Wg', 'L0_conv_bg', 'L0_conv_W1', 'L0_conv_b1', 'L0_conv_W2', 'L0_conv_b2',
        'L1_attn_w_attn', 'L1_attn_b_attn', 'L1_attn_w_proj', 'L1_attn_b_proj',
        'L1_ffn_gate_w', 'L1_ffn_gate_b', 'L1_ffn_w1', 'L1_ffn_b1', 'L1_ffn_w2', 'L1_ffn_b2']


def kernel(**inputs):
    import numpy as _np
    import concourse.bacc as _bacc
    from concourse import mybir as _mybir
    from concourse.bass_utils import run_bass_kernel_spmd as _run

    nc = _bacc.Bacc("TRN2", target_bir_lowering=False, num_devices=1)
    arrays, args = {}, []
    for name in _INS:
        a = _np.ascontiguousarray(inputs[name])
        arrays[f"in_{name}_dram"] = a
        args.append(nc.dram_tensor(f"in_{name}_dram", a.shape, _mybir.dt.from_np(a.dtype), kind="ExternalInput").ap())
    args.append(nc.dram_tensor("out_dram", (NIMG, 32, 32, D), _mybir.dt.float32, kind="ExternalOutput").ap())
    build(nc, *args)
    r = _run(nc, [arrays], core_ids=[0])
    return r.results[0]["out_dram"]
```
